# Optimizing a Trainium2 kernel written in Bass

```python
import numpy as np
import jax
import jax.numpy as jnp

def _softmax(x, axis=-1):
    return jax.nn.softmax(x, axis=axis)

def _gelu(x):
    return jax.nn.gelu(x, approximate=True)

def _silu(x):
    return jax.nn.silu(x)

def _sigmoid(x):
    return jax.nn.sigmoid(x)

def _layernorm(x, axis=-1, eps=1e-05):
    m = jnp.mean(x, axis=axis, keepdims=True)
    v = jnp.var(x, axis=axis, keepdims=True)
    return (x - m) / jnp.sqrt(v + eps)

def _scatter_add(tgt, idx, src, axis=0):
    return tgt.at[idx].add(src)

def _segment_sum(src, seg, n):
    return jax.ops.segment_sum(src, seg, n)
kernel_name = 'mk_conv_attn_hybrid_d2_conv_nhwc256_r4_418cd7'

def setup_inputs(seed: int=0):
    np.random.seed(seed)
    _w = jnp.asarray

    def _rec_inputs():
        import jax
        import jax.numpy as jnp
        _gk = jax.random.key(seed)
        x = -0.0002091 + 1 * jax.random.normal(jax.random.fold_in(_gk, 1), (32, 56, 56, 64), jnp.float32)
        return x
    x = _rec_inputs()

    def _L0_conv_setup():
        import jax, jax.numpy as jnp
        import numpy as np
        EPSILON = 0.001
        key = jax.random.key(seed)
        k1, k2 = jax.random.split(key)
        x = jax.random.normal(k1, (32, 56, 56, 64), dtype=jnp.float32)
        kernel = jax.random.normal(k2, (3, 3, 64, 64), dtype=jnp.float32) * 0.05
        return {'x': x, 'kernel': kernel}
    _L0_conv_all = _L0_conv_setup()
    _L0_conv_in = {k: v for k, v in _L0_conv_all.items() if k in ('kernel',)}
    del _L0_conv_all

    def _L1_attn_setup():
        import jax, jax.numpy as jnp
        import numpy as np
        import math
        N, HW, D = (8, 4096, 64)
        HEADS = 8
        key = jax.random.key(seed)
        ks = jax.random.split(key, 9)
        s = 1.0 / math.sqrt(D)
        return {'x': jax.random.normal(ks[0], (N, HW, D), jnp.float32), 'Wk': jax.random.normal(ks[1], (D, D), jnp.float32) * s, 'bk': jax.random.normal(ks[2], (D,), jnp.float32) * 0.01, 'Wq': jax.random.normal(ks[3], (D, D), jnp.float32) * s, 'bq': jax.random.normal(ks[4], (D,), jnp.float32) * 0.01, 'Wv': jax.random.normal(ks[5], (D, D), jnp.float32) * s, 'bv': jax.random.normal(ks[6], (D,), jnp.float32) * 0.01, 'Wr': jax.random.normal(ks[7], (D, D), jnp.float32) * s, 'br': jax.random.normal(ks[8], (D,), jnp.float32) * 0.01}
    _L1_attn_all = _L1_attn_setup()
    _L1_attn_in = {k: v for k, v in _L1_attn_all.items() if k in ('Wk', 'bk', 'Wq', 'bq', 'Wv', 'bv', 'Wr', 'br')}
    del _L1_attn_all

    def _L1_ffn_setup():
        import jax, jax.numpy as jnp
        import numpy as np
        TOP_K = 2
        key = jax.random.key(seed)
        ks = jax.random.split(key, 4)
        B, L, D, H, E = (8, 1024, 64, 256, 8)
        s = 0.02
        return {'x': jax.random.normal(ks[0], (B, L, D), jnp.float32), 'Wg': jax.random.normal(ks[1], (D, E), jnp.float32) * s, 'bg': jnp.zeros((E,), jnp.float32), 'W1': jax.random.normal(ks[2], (E, D, H), jnp.float32) * s, 'b1': jnp.zeros((E, H), jnp.float32), 'W2': jax.random.normal(ks[3], (E, H, D), jnp.float32) * s, 'b2': jnp.zeros((E, D), jnp.float32)}
    _L1_ffn_all = _L1_ffn_setup()
    _L1_ffn_in = {k: v for k, v in _L1_ffn_all.items() if k in ('Wg', 'bg', 'W1', 'b1', 'W2', 'b2')}
    del _L1_ffn_all
    return {'x': x, 'L0_conv_kernel': _L0_conv_in['kernel'], 'L1_attn_Wk': _L1_attn_in['Wk'], 'L1_attn_bk': _L1_attn_in['bk'], 'L1_attn_Wq': _L1_attn_in['Wq'], 'L1_attn_bq': _L1_attn_in['bq'], 'L1_attn_Wv': _L1_attn_in['Wv'], 'L1_attn_bv': _L1_attn_in['bv'], 'L1_attn_Wr': _L1_attn_in['Wr'], 'L1_attn_br': _L1_attn_in['br'], 'L1_ffn_Wg': _L1_ffn_in['Wg'], 'L1_ffn_bg': _L1_ffn_in['bg'], 'L1_ffn_W1': _L1_ffn_in['W1'], 'L1_ffn_b1': _L1_ffn_in['b1'], 'L1_ffn_W2': _L1_ffn_in['W2'], 'L1_ffn_b2': _L1_ffn_in['b2']}

def reference(x, L0_conv_kernel, L1_attn_Wk, L1_attn_bk, L1_attn_Wq, L1_attn_bq, L1_attn_Wv, L1_attn_bv, L1_attn_Wr, L1_attn_br, L1_ffn_Wg, L1_ffn_bg, L1_ffn_W1, L1_ffn_b1, L1_ffn_W2, L1_ffn_b2):
    import jax
    import jax.numpy as jnp

    def _L0_conv_ref(x, kernel):
        import jax, jax.numpy as jnp
        import numpy as np
        EPSILON = 0.001
        binary_kernel = kernel * (1.0 + EPSILON) / (jnp.abs(kernel) + EPSILON)
        out = jax.lax.conv_general_dilated(x, binary_kernel, window_strides=(1, 1), padding='SAME', rhs_dilation=(1, 1), dimension_numbers=('NHWC', 'HWIO', 'NHWC'))
        return jax.nn.relu(out)

    def _L1_attn_ref(x, Wk, bk, Wq, bq, Wv, bv, Wr, br):
        import jax, jax.numpy as jnp
        import numpy as np
        import math
        N, HW, D = (8, 4096, 64)
        HEADS = 8
        n, hw, d = x.shape
        heads = HEADS
        hk = d // heads
        hv = d // heads
        flat = x.reshape(n, d, hw)
        keys = jnp.einsum('kd,ndl->nkl', Wk, flat) + bk[None, :, None]
        queries = jnp.einsum('kd,ndl->nkl', Wq, flat) + bq[None, :, None]
        values = jnp.einsum('vd,ndl->nvl', Wv, flat) + bv[None, :, None]
        K = jax.nn.softmax(keys.reshape(n, heads, hk, hw), axis=3)
        Q = jax.nn.softmax(queries.reshape(n, heads, hk, hw), axis=2)
        V = values.reshape(n, heads, hv, hw)
        context = jnp.einsum('nhkl,nhvl->nhkv', K, V)
        att = jnp.einsum('nhkv,nhkl->nhvl', context, Q)
        agg = att.reshape(n, heads * hv, hw)
        out = jnp.einsum('dv,nvl->ndl', Wr, agg) + br[None, :, None]
        return out.reshape(n, hw, d)

    def _L1_ffn_ref(x, Wg, bg, W1, b1, W2, b2):
        import jax, jax.numpy as jnp
        import numpy as np
        TOP_K = 2
        B, L, D = x.shape
        E = W1.shape[0]
        xf = x.reshape(-1, D)
        gate_logits = xf @ Wg + bg
        top_w, top_i = jax.lax.top_k(gate_logits, TOP_K)
        top_w = jax.nn.softmax(top_w, axis=-1)
        w_dense = jnp.sum(jax.nn.one_hot(top_i, E, dtype=xf.dtype) * top_w[..., None], axis=1)
        out = jnp.zeros_like(xf)
        for e in range(E):
            h = jax.nn.gelu(xf @ W1[e] + b1[e], approximate=False)
            out = out + w_dense[:, e:e + 1] * (h @ W2[e] + b2[e])
        return out.reshape(B, L, D)

    def _gn(v, G=32, eps=1e-05):
        B_, H_, W_, C_ = v.shape
        g = v.reshape(B_, H_, W_, G, C_ // G)
        m = jnp.mean(g, axis=(1, 2, 4), keepdims=True)
        s = jnp.var(g, axis=(1, 2, 4), keepdims=True)
        return ((g - m) / jnp.sqrt(s + eps)).reshape(v.shape)

    def _ln_c(v, eps=1e-06):
        m = jnp.mean(v, axis=-1, keepdims=True)
        s = jnp.var(v, axis=-1, keepdims=True)
        return (v - m) / jnp.sqrt(s + eps)

    def _ln_t(v, eps=1e-05):
        m = jnp.mean(v, axis=-1, keepdims=True)
        s = jnp.var(v, axis=-1, keepdims=True)
        return (v - m) / jnp.sqrt(s + eps)

    def _to_tokens(v):
        B_, H_, W_, C_ = v.shape
        return v.reshape(B_, H_ * W_, C_)

    def _from_tokens(t, like):
        return t.reshape(like.shape)
    x = x + _L0_conv_ref(_gn(x), L0_conv_kernel)
    t = _to_tokens(x)
    t = t + _L1_attn_ref(_ln_t(t), L1_attn_Wk, L1_attn_bk, L1_attn_Wq, L1_attn_bq, L1_attn_Wv, L1_attn_bv, L1_attn_Wr, L1_attn_br)
    t = t + _L1_ffn_ref(_ln_t(t), L1_ffn_Wg, L1_ffn_bg, L1_ffn_W1, L1_ffn_b1, L1_ffn_W2, L1_ffn_b2)
    x = _from_tokens(t, x)
    return x

_drawn_inputs = setup_inputs


def setup_inputs(seed=0):
    import zlib

    import numpy as np

    out = dict(_drawn_inputs(seed))
    spreads = {'L1_ffn_bg': (0.0, 2.0), 'L1_ffn_b1': (0.0, 2.0), 'L1_ffn_b2': (0.0, 2.0)}
    factors = {'L1_attn_Wk': 8.0,
     'L1_attn_bk': 200.0,
     'L1_attn_Wq': 8.0,
     'L1_attn_bq': 23.12,
     'L1_attn_Wv': 8.0,
     'L1_attn_bv': 32.931,
     'L1_attn_Wr': 8.0,
     'L1_attn_br': 200.0,
     'L1_ffn_Wg': 8.0,
     'L1_ffn_W1': 8.0,
     'L1_ffn_W2': 8.0}
    for name, (base, spread) in spreads.items():
        noise = np.random.default_rng([zlib.crc32(name.encode()), seed]).standard_normal(out[name].shape)
        drawn = base * np.exp(spread * noise) if base else spread * noise
        out[name] = jnp.asarray(drawn.astype(out[name].dtype))
    for name, factor in factors.items():
        out[name] = (out[name] * factor).astype(out[name].dtype)
    return out
```

```python
from contextlib import ExitStack

import concourse.bass as bass
from concourse import mybir

F32 = mybir.dt.float32
F32R = mybir.dt.float32r
ALU = mybir.AluOpType
ACT = mybir.ActivationFunctionType
AX = mybir.AxisListType

IMAGES, HW, C = 32, 56, 64
PAIRS = IMAGES // 2
TOKENS = HW * HW
J = TOKENS // 64
NB = 7
JB = J // NB
BL = JB * 64
ROWS = HW // NB
TQ, TR = 112, 28
LC = 112
CH = BL // LC
NCH = NB * CH
PADW, PADH = HW + 2, HW + 1
E, HID = 8, 256
NQ = E * HID // 128
HB = 4
EPS = 1e-5
CONV_EPS = 0.001
GROUPS = 64 // 8
NEG = -3.0e38
JG = ((0, 4), (4, 7))


def plan():
    steps = []

    def at(slot, name, *args, behind=0):
        steps.append((slot, len(steps), name, args, behind))

    for s in range(NB * NQ):
        b, q = divmod(s, NQ)
        at(s, "ffn", b, q, behind=1)
        if q % 2 == 1:
            at(s, "y", b, q // 2, behind=1)
        if q == 3 and b >= 1:
            at(s, "fin", b - 1, behind=1)
    last = NB * NQ
    at(last, "fin", NB - 1, behind=1)

    def post(b, xf, behind=0):
        at(xf, "xf", b, 0, behind=behind)
        at(xf + 1, "xf", b, 1, behind=behind)
        at(xf + 3, "lg", b, behind=behind)
        at(xf + 4, "gate_a", b, behind=behind)
        at(xf + 6, "gate_b", b, behind=behind)
        at(xf + 8, "wt", b, 0, behind=behind)
        at(xf + 9, "wt", b, 1, behind=behind)

    post(NB - 1, 0, behind=1)
    t = 10
    for k in range(14):
        at(t + k, "tx", k // 7, k % 7)
        if k in (6, 13):
            at(t + k, "xr_free", k // 7)
    at(t + 14, "stats")
    at(t + 16, "gs")
    at(t + 17, "norm")
    t = 29
    for b in range(NB):
        at(t + 3 * b // 2, "cv", b)
    t = 40
    for b in range(NB):
        s = t + 2 * b
        at(s, "yt", b, 0)
        at(s + 1, "yt", b, 1)
        at(s + 1, "ln_a", 0, b)
        at(s + 2, "ln_b", 0, b)
        at(s + 3, "ln_c", 0, b)
    for b in range(NB):
        s = t + 4 + 2 * b
        at(s - .5, "k", b)
        at(s, "qv", b, 0)
        at(s + .5, "qv", b, 1)
        at(s + 2, "qs", b)
        at(s + 3.5, "qb", b)
    steps.sort(key=lambda x: (x[0], x[1]))
    t = 58
    at(t, "kmax")
    t = 62
    at(t, "exp")
    for b in range(NB):
        at(t + 1 + b, "kt", b)
        at(t + 1 + b, "sq", b)
    at(t + 8, "ksum")
    at(t + 9, "ctx")
    at(t + 11, "m")
    t = 75
    for b in range(NB):
        at(t + b, "out", b)
        at(t + 2 + 2 * b, "ln_a", 1, b)
        at(t + 3 + 2 * b, "ln_b", 1, b)
        at(t + 4 + 2 * b, "ln_c", 1, b)
        at(t + 5 + 2 * b, "hl", b)
    for b in range(NB - 2):
        post(b, t + 7 + 2 * b)
    post(NB - 2, 98)
    for b in range(NB - 1):
        at(106, "res", b)
    at(last, "res", NB - 1)
    steps.sort(key=lambda x: (x[0], x[1]))
    return [(name, args, behind) for _, _, name, args, behind in steps]


SCHEDULE = plan()
PRE_KINDS = ("tx", "gs", "cv", "yt", "k", "qv", "qb", "kt", "sq", "ctx", "m", "out", "xf", "lg", "wt")
PRE_FILLS = [(s[0],) + s[1] for d in (0, 1) for s in SCHEDULE if s[0] in PRE_KINDS and s[2] == d]
PRE_FILLS += ["pad"] * (len(PRE_FILLS) % 2)
FFN_FILLS = [("wb", 0, 0)]
for _name, _args, _ in SCHEDULE:
    if _name == "ffn" and _args[1] % 2 == 0 and (_args[0], _args[1] // 2) != (NB - 1, E - 1):
        _x = _args[0] * E + _args[1] // 2 + 1
        FFN_FILLS.append(("wb", _x // E, _x % E))
    if _name == "fin":
        FFN_FILLS.append(("fin",) + _args)


def build_program(nc, x, conv, Wk, bk, Wq, bq, Wv, bv, Wr, br, Wg, bg, W1, b1, W2, b2, out):
    ctx = ExitStack()
    with ctx:
        def sb(name, shape, dt=F32):
            return ctx.enter_context(nc.sbuf_tensor(name, shape, dt))

        def sem(name):
            return ctx.enter_context(nc.semaphore(name))

        x_tok = sb("x_tok", [128, J, C])
        raw_kt = sb("raw_kt", [128, TR, 128])
        pad_qv = sb("pad_qv", [128, NB * BL + NCH * 128])
        xpad = pad_qv[:, 0:2 * PADH * PADW].rearrange("p (i r w) -> p i r w", i=2, r=PADH)
        Q = pad_qv[:, 0:NB * BL]
        VT = pad_qv[:, NB * BL:].rearrange("p (h k) -> p h k", k=128)
        conv_y = sb("conv_y", [128, TOKENS])
        keys = sb("keys", [128, TOKENS])
        ln_x = sb("ln_x", [128, 2, JB, C])
        ln_sq = sb("ln_sq", [128, JB, C])
        ln_s = sb("ln_s", [128, 2, 5, JB])
        QT = sb("QT", [LC, 2, CH, 128])
        q_max = sb("q_max", [LC, 2, CH * 16])
        q_rec = conv_y[:, 0:2 * BL].rearrange("p (r l) -> p r l", r=2)
        xhl = sb("xhl", [128, 2, JB, 2, C])
        xT = sb("xT", [128, J, 128], F32R)
        wT = sb("wT", [128, J, 64], F32R)
        res = sb("res", [128, J, C])
        h_sb = sb("h_sb", [128, HB, 2, BL])
        wb_sb = sb("wb_sb", [128, 2, BL])
        y_tmp = sb("y_tmp", [128, 2, BL])
        acc = sb("acc", [128, 2, JB, 64])
        out_sb = sb("out_sb", [128, 2, JB, C])
        W1hi = sb("W1hi", [128, E * HID], F32R)
        W1lo = sb("W1lo", [128, E * HID], F32R)
        W2s = sb("W2s", [128, NQ, C])
        Wghi = sb("Wghi", [128, E], F32R)
        Wglo = sb("Wglo", [128, E], F32R)
        conv_w = sb("conv_w", [128, 6, C])
        WT4 = sb("WT4", [128, 4, 128])
        sel = sb("sel", [128, E, 128], F32R)
        ident = sb("ident", [128, 128])
        head_mask = sb("head_mask", [128, 128])
        pair_mean = sb("pair_mean", [128, 128])
        pair_diff = sb("pair_diff", [128, 128])
        ctx_m = sb("ctx_m", [128, 128])
        mix = sb("mix", [128, 128])
        bqv = sb("bqv", [LC, 256])
        bkr = sb("bkr", [128, 2])
        b1T = sb("b1T", [128, NQ])
        b2T = sb("b2T", [128, E])
        bg_sb = sb("bg_sb", [128, E])
        rev = sb("rev", [128, E])
        bns = sb("bns", [128, 2, NB, 6])
        gn = sb("gn", [128, 20])
        mhalf = sb("mhalf", [128, JB])
        euler = sb("euler", [128, JB])
        kst = sb("kst", [128, 2, NB])
        kred = sb("kred", [128, 3])
        lg = sb("lg", [128, 6, JB, E])
        gs7 = sb("gs7", [128, 9, JB])
        w32 = sb("w32", [128, 2, JB, 32])
        w1_raw = keys[:, 0:E * HID]
        sel_raw = conv_y[:, 0:E * 128].rearrange("p (e m) -> p e m", e=E)
        w_raw = conv_y[:, E * 128:E * 128 + 512].rearrange("p (w m) -> p w m", w=4)
        conv_raw = conv_y[:, 1536:1536 + 384].rearrange("p (w m) -> p w m", w=6)
        conv_abs = conv_y[:, 1920:1920 + 384].rearrange("p (w m) -> p w m", w=6)
        wg_raw = conv_y[:, 2304:2304 + E]
        KT = raw_kt

        psum = ctx.enter_context(nc.psum_tensor("psum", [128, 8, 512], F32))
        PRE0, YB, FB = 4, 6, 7

        def sems(names):
            return {name: sem(name) for name in names.split()}

        S = sems("weights_loaded consts_pool consts_dve weights_t x_loaded raw_loaded0 raw_loaded1 "
                 "pre_full0 pre_full1 pre_free0 pre_free1 ffn_full ffn_free "
                 "h_full h_ready h_used y_free acc_added out_stored0 out_stored1 res_copied "
                 "gn_dve gn_pool ln_dve ln_pool hi_dve hl_pool qs_dve kmax_dve exp_act qmul_pool "
                 "gate_dve gate_pool mask_dve")

        PER = dict(x_loaded=16, raw_loaded0=32, raw_loaded1=32,
                   pre_full0=len(PRE_FILLS) // 2, pre_full1=len(PRE_FILLS) // 2,
                   pre_free0=len(PRE_FILLS) // 2, pre_free1=len(PRE_FILLS) // 2,
                   ffn_full=len(FFN_FILLS), ffn_free=len(FFN_FILLS),
                   h_full=NB * NQ, h_ready=NB * NQ, h_used=NB * NQ, y_free=NB * E,
                   acc_added=NB * (E - 1), out_stored0=16 * 4, out_stored1=16 * 3, res_copied=NB,
                   gn_dve=10, gn_pool=1, ln_dve=2 * NB * 6, ln_pool=2 * NB * 2, hi_dve=NB, hl_pool=NB,
                   qs_dve=2 * NB, kmax_dve=3, exp_act=2 * NB, qmul_pool=NB,
                   gate_dve=20 * NB, gate_pool=NB)

        def at(name, n, c):
            value = n * PER[name] + max(c, 0)
            return S[name], max(value, 0) if isinstance(value, int) else value

        def pre_bank(*fill):
            k = PRE_FILLS.index(fill)
            return PRE0 + k % 2, k

        def bank_of(*fill):
            return psum[:, pre_bank(*fill)[0], :]

        def filled(n, *fill):
            k = PRE_FILLS.index(fill)
            return at(f"pre_full{k % 2}", n, k // 2 + 1)

        def drained(n, *fills, by=None):
            last = {}
            for fill in fills:
                k = PRE_FILLS.index(fill)
                last[k % 2] = max(k // 2, last.get(k % 2, 0))
            return [at(f"pre_free{bank}", n, k + 1) for bank, k in last.items()
                    if by is None or PRE_FILLS.index(by) % 2 != bank]

        def pre_free(fill):
            return S[f"pre_free{pre_bank(*fill)[1] % 2}"]

        xp = x.rearrange("(n i) h w c -> n i (h w c)", i=2)
        op = out.rearrange("(n i) h w c -> n i (h w c)", i=2)

        def turns(eng, pre, ffn):
            def turn(n, front, back):
                for name, args, behind in SCHEDULE:
                    if (behind and back) or (not behind and front):
                        step = ffn if name in ("ffn", "y", "fin") else pre
                        step(n - behind, name, *args)

            turn(0, True, False)
            turn(1, True, True)
            with eng.Fori(2, PAIRS) as n:
                turn(n, True, True)
            turn(PAIRS, False, True)

        block = ctx.enter_context(nc.Block())

        @block.sync
        def _(sp):
            loads = 0

            def load(dst, src):
                nonlocal loads
                sp.dma_start(dst, src, allow_slow_non_contiguous=True).then_inc(S["weights_loaded"], 16)
                loads += 1

            sp.wait_ge(S["consts_dve"], 2)
            for i in range(2):
                h = slice(64 * i, 64 * i + 64)
                for w, mat in enumerate((Wq, Wv, Wk, Wr)):
                    load(w_raw[h, w, h], mat)
                load(w1_raw[h, :].rearrange("d (e h) -> d e h", e=E), W1.rearrange("e d h -> d e h"))
                load(wg_raw[h, :], Wg)
                load(bkr[h, 0:1], bk.rearrange("(c o) -> c o", o=1))
                load(bkr[h, 1:2], br.rearrange("(c o) -> c o", o=1))
                load(b2T[h, :], b2.rearrange("e c -> c e"))
                load(bqv[:, h], bq.unsqueeze(0).to_broadcast([LC, 64]))
                load(bqv[:, 128 + 64 * i:192 + 64 * i], bv.unsqueeze(0).to_broadcast([LC, 64]))
                load(conv_raw[h, 0:3, :], conv[i].rearrange("x ci co -> ci x co"))
            load(conv_raw[64:128, 3:6, :], conv[2].rearrange("x ci co -> ci x co"))
            load(W2s[:, :, :], W2.rearrange("e (k p) c -> p (e k) c", p=128))
            load(b1T[:, :], b1.rearrange("e (k p) -> p (e k)", p=128))
            load(bg_sb[:, :], bg.unsqueeze(0).to_broadcast([128, E]))
            assert loads == WEIGHT_LOADS

            def row(n):
                return n if isinstance(n, int) else bass.ds(n, 1)

            def pre(n, name, *a):
                if name == "tx" and a == (0, 0):
                    sp.wait_ge(*filled(n - 1, "ctx"))
                    load_raw_at(n, 0)
                    sp.wait_ge(*at("res_copied", n - 1, NB))
                    load_tok_at(n)
                if name == "xr_free" and a == (0,):
                    sp.wait_ge(*filled(n, "tx", 0, 6))
                    load_raw_at(n, 1)

            def load_raw_at(n, i):
                src = xp[row(n), i]
                if not isinstance(n, int):
                    src = src.rearrange("o m -> (o m)")
                body = src.rearrange("(q r c) -> q r c", q=TQ, r=TR)
                sp.dma_start(raw_kt[0:TQ, :, 64:128], body).then_inc(S[f"raw_loaded{i}"], 16)
                sp.dma_start(raw_kt[2:TQ, :, 0:64], body[0:TQ - 2]).then_inc(S[f"raw_loaded{i}"], 16)

            def load_tok_at(n):
                src = xp[row(n)]
                if not isinstance(n, int):
                    src = src.rearrange("o i m -> (o i) m")
                sp.dma_start(x_tok[:, :, :], src.rearrange("i (p j c) -> (i p) j c", p=64, c=C)) \
                    .then_inc(S["x_loaded"], 16)

            def ffn(n, name, *a):
                if name == "fin":
                    b = a[0]
                    sp.wait_ge(*at("ffn_free", n, FFN_FILLS.index(("fin", b)) + 1))
                    dst = op[row(n)]
                    if not isinstance(n, int):
                        dst = dst.rearrange("o i m -> (o i) m")
                    dst = dst.rearrange("i (p j c) -> (i p) j c", p=64, c=C)
                    sp.dma_start(dst[:, JB * b:JB * b + JB, :], out_sb[:, b % 2, :, :]).then_inc(S[f"out_stored{b % 2}"], 16)

            turns(sp, pre, ffn)
            sp.wait_ge(*at("out_stored0", PAIRS, 0))
            sp.wait_ge(*at("out_stored1", PAIRS, 0))

        @block.gpsimd
        def _(pool):
            count = 0

            def const(ins):
                nonlocal count
                count += 1
                ins.then_inc(S["consts_pool"], 1)
                pool.wait_ge(S["consts_pool"], count)

            const(pool.memset(ident[:, :], 0.0))
            const(pool.affine_select(out=ident[:, :], in_=ident[:, :], compare_op=ALU.not_equal, fill=1.0,
                                     base=0, pattern=[[-1, 128]], channel_multiplier=1))
            const(pool.memset(head_mask[:, :], 1.0))
            hm = head_mask[:, :].rearrange("p (g k) -> p g k", k=GROUPS)
            const(pool.affine_select(out=hm, in_=hm, compare_op=ALU.is_ge, fill=0.0, base=0,
                                     pattern=[[-GROUPS, 16], [0, GROUPS]], channel_multiplier=1))
            const(pool.affine_select(out=hm, in_=hm, compare_op=ALU.is_ge, fill=0.0, base=GROUPS - 1,
                                     pattern=[[GROUPS, 16], [0, GROUPS]], channel_multiplier=-1))
            const(pool.memset(pair_mean[:, :], 0.0))
            const(pool.memset(pair_diff[:, :], 0.0))
            for m, signs in ((pair_mean, (0.5, 0.5)), (pair_diff, (0.5, -0.5))):
                for half in range(2):
                    for u in range(2):
                        v = m[64:128, 64 * half:64 * half + 64].rearrange("p (g u) -> p g u", u=2)
                        const(pool.affine_select(out=v, in_=v, compare_op=ALU.not_equal, fill=signs[u], base=-u,
                                                 pattern=[[-2, 32], [0, 2]], channel_multiplier=1))
            pool.wait_ge(S["consts_dve"], 2)
            for i in range(2):
                for part in range(2):
                    v = sel_raw[64 * i:64 * i + 64, :, 64 * i:64 * i + 64]
                    const(pool.affine_select(out=v, in_=v, compare_op=ALU.not_equal, fill=1.0, base=-E * part,
                                             pattern=[[-1, E], [0, 64]], channel_multiplier=1))
            assert count == POOL_CONSTS

            def ln_at(layer, b):
                return layer * NB + b

            def pre(n, name, *a):
                if name == "gs":
                    pool.wait_ge(*at("gn_dve", n, 6))
                    pool.tensor_tensor(gn[:, 14:16], gn[:, 12:14], mhalf[:, 0:2], ALU.pow).then_inc(S["gn_pool"], 1)
                elif name == "ln_a":
                    k = ln_at(*a)
                    pool.wait_ge(*at("ln_dve", n, 6 * k + 3))
                    pool.wait_ge(*at("ln_dve", n, 6 * k - 2))
                    xc = ln_x[:, k % 2, :, :]
                    pool.tensor_tensor(ln_sq[:, :, :], xc, xc, ALU.mult).then_inc(S["ln_pool"], 1)
                elif name == "ln_b":
                    k = ln_at(*a)
                    pool.wait_ge(*at("ln_dve", n, 6 * k + 5))
                    pool.tensor_tensor(ln_s[:, k % 2, 4, :], ln_s[:, k % 2, 3, :], mhalf[:, :], ALU.pow) \
                        .then_inc(S["ln_pool"], 1)
                elif name == "hl":
                    b = a[0]
                    k = ln_at(1, b)
                    pool.wait_ge(*at("hi_dve", n, b + 1))
                    pool.tensor_tensor(xhl[:, b % 2, :, 1, :].bitcast(F32R), ln_x[:, k % 2, :, :],
                                       xhl[:, b % 2, :, 0, :], ALU.subtract).then_inc(S["hl_pool"], 1)
                elif name == "sq":
                    b = a[0]
                    for free in drained(n, ("sq", b)):
                        pool.wait_ge(*free)
                    qb = Q[:, BL * b:BL * b + BL]
                    pool.tensor_tensor(qb, qb, q_rec[:, b % 2, :], ALU.mult).then_inc(S["qmul_pool"], 1)
                elif name == "gate_a":
                    b = a[0]
                    pool.wait_ge(*at("gate_dve", n, 20 * b + 12))
                    pool.tensor_tensor(gs7[:, 5, :], euler[:, :], gs7[:, 4, :], ALU.pow).then_inc(S["gate_pool"], 1)

            def ffn(n, name, *a):
                if name == "y" and a[1] >= 1:
                    b, e = a
                    pool.wait_ge(*at("y_free", n, b * E + e + 1))
                    pool.wait_ge(*at("acc_added", n, b * (E - 1) + e - 1))
                    s = acc[:, b % 2, :, :].rearrange("p j c -> p (j c)")
                    pool.tensor_tensor(s, s, y_tmp[:, e % 2, :], ALU.add).then_inc(S["acc_added"], 1)

            turns(pool, pre, ffn)

        @block.scalar
        def _(act):
            act.wait_ge(S["weights_loaded"], 16 * WEIGHT_LOADS)

            def pre(n, name, *a):
                if name == "tx":
                    i, g = a
                    act.wait_ge(*filled(n, name, *a))
                    src = bank_of(name, *a)
                    if a == (0, 0):
                        act.wait_ge(*filled(n - 1, "out", NB - 1))
                        act.wait_ge(*filled(n - 1, "ctx"))
                    dst = xpad[:, i, 0:HW, 1:1 + HW].rearrange("p r (h q) -> p r h q", h=2)[:, :, :, 4 * g:4 * g + 4]
                    act.copy(dst, src[:, 0:448].rearrange("p (k r h) -> p r h k", k=4, h=2)) \
                        .then_inc(pre_free((name,) + a), 1)
                elif name == "cv":
                    b = a[0]
                    act.wait_ge(*filled(n, name, b))
                    src = bank_of(name, b)
                    if b == 0:
                        act.wait_ge(*filled(n - 1, "yt", NB - 1, 1))
                    act.activation(conv_y[:, BL * b:BL * b + BL], src[:, 0:BL], ACT.Relu) \
                        .then_inc(pre_free((name,) + a), 1)
                elif name == "qb":
                    b = a[0]
                    act.wait_ge(*filled(n, name, b))
                    src = bank_of(name, b)
                    act.copy(Q[:, BL * b:BL * b + BL], src[:, 0:BL]).then_inc(pre_free((name,) + a), 1)
                elif name == "exp":
                    act.wait_ge(*at("kmax_dve", n, 1))
                    for b in range(NB):
                        kb = keys[:, BL * b:BL * b + BL]
                        act.activation(kb, kb, ACT.Exp, bias=kred[:, 0:1], accum_out=kst[:, 1, b:b + 1]) \
                            .then_inc(S["exp_act"], 1)
                    for free in drained(n, ("qb", NB - 1), ("qb", NB - 2)):
                        act.wait_ge(*free)
                    for b in range(NB):
                        qb = Q[:, BL * b:BL * b + BL]
                        act.activation(qb, qb, ACT.Exp).then_inc(S["exp_act"], 1)
                elif name == "xf":
                    b, g = a
                    j0, j1 = JG[g]
                    act.wait_ge(*filled(n, name, b, g))
                    src = bank_of(name, b, g)
                    act.wait_ge(*at("h_full", n - 1, NQ * (b + 1)))
                    act.copy(xT[:, JB * b + j0:JB * b + j1, :], src[:, 0:128 * (j1 - j0)].rearrange(
                        "p (j t) -> p j t", t=128)).then_inc(pre_free((name,) + a), 1)

            def wb(n, b, e):
                k = FFN_FILLS.index(("wb", b, e))
                act.wait_ge(*at("ffn_full", n, k + 1))
                act.wait_ge(*at("y_free", n, b * E + e - 1))
                act.copy(wb_sb[:, e % 2, :], psum[:, FB, 0:BL]).then_inc(S["ffn_free"], 1)

            def gelu(n, s):
                act.wait_ge(*at("h_full", n, s + 1))
                act.wait_ge(*at("h_used", n, s + 1 - HB))
                act.activation(h_sb[:, s % HB, :, :],
                               psum[:, 2 * (s % 2):2 * (s % 2) + 2, 0:BL], ACT.Gelu,
                               bias=b1T[:, s % NQ:s % NQ + 1]).then_inc(S["h_ready"], 1)

            def ffn(n, name, *a):
                if name == "ffn":
                    b, q = a
                    s = b * NQ + q
                    if s == 0:
                        gelu(n, 0)
                        wb(n, 0, 0)
                    if s + 1 < NB * NQ:
                        gelu(n, s + 1)
                    if q % 2 == 0 and (b, q // 2) != (NB - 1, E - 1):
                        x = b * E + q // 2 + 1
                        wb(n, x // E, x % E)

            turns(act, pre, ffn)

        @block.tensor
        def _(pe):
            pe.wait_ge(S["consts_pool"], POOL_CONSTS)
            pe.wait_ge(S["weights_loaded"], 16 * WEIGHT_LOADS)
            for w in range(4):
                ins = pe.transpose(psum[:, 0, 128 * w:128 * w + 128], w_raw[:, w, :], ident[:, :])
            ins.then_inc(S["weights_t"], 1)
            pe.wait_ge(S["consts_dve"], DVE_CONSTS)

            def bank_for(n, *fill):
                bank, k = pre_bank(*fill)
                pe.wait_ge(*at(f"pre_free{k % 2}", n, k // 2))
                return psum[:, bank, :], S[f"pre_full{k % 2}"]

            def pre(n, name, *a):
                if name not in PRE_KINDS:
                    return
                dst, full = bank_for(n, name, *a)
                if name == "tx":
                    i, g = a
                    if g == 0:
                        pe.wait_ge(*at(f"raw_loaded{i}", n, 32))
                    for r in range(4):
                        ins = pe.transpose(dst[:, TQ * r:TQ * r + TQ], raw_kt[0:TQ, 4 * g + r, :],
                                           ident[0:TQ, 0:TQ])
                elif name == "gs":
                    pe.wait_ge(*at("gn_dve", n, 4))
                    pe.matmul(dst[:, 0:4], pair_mean[:, :], gn[:, 0:4], start=True, stop=True)
                    ins = pe.matmul(dst[:, 4:8], pair_diff[:, :], gn[:, 0:4], start=True, stop=True)
                elif name == "cv":
                    b = a[0]
                    pe.wait_ge(*at("gn_dve", n, 10))
                    for t in range(6):
                        r0, dx = ROWS * b + t // 3, t % 3
                        for i in range(2):
                            ins = pe.matmul(dst[64 * i:64 * i + 64, 0:BL], conv_w[:, t, :],
                                            xpad[:, i, r0:r0 + ROWS, dx:dx + HW], start=(t == 0), stop=(t == 5))
                elif name == "yt":
                    b, g = a
                    for free in drained(n, ("cv", NB - 1), ("cv", NB - 2), by=(name,) + a):
                        pe.wait_ge(*free)
                    cols = conv_y[:, :].rearrange("k (p j) -> k j p", j=J)
                    for j in range(*JG[g]):
                        o = 128 * (j - JG[g][0])
                        if o == 0:
                            ins = pe.matmul(dst[0:64, o:o + 128], cols[:, JB * b + j, :], ident[:, :],
                                            start=True, stop=True)
                        else:
                            ins = pe.transpose(dst[0:64, o:o + 128], cols[:, JB * b + j, :], ident[:, :])
                elif name == "k":
                    b = a[0]
                    pe.wait_ge(*at("ln_dve", n, 6 * b + 6))
                    ins = pe.matmul(dst[:, 0:BL], WT4[:, 2, :], ln_x[:, b % 2, :, :].rearrange("p j c -> p (j c)"),
                                    start=True, stop=True)
                elif name == "qv":
                    b, g = a
                    pe.wait_ge(*at("ln_dve", n, 6 * b + 6))
                    t = ln_x[:, b % 2, :, :].rearrange("p j c -> p (j c)")
                    for c in range(2):
                        o = LC * (2 * g + c)
                        ins = pe.matmul(dst[0:LC, 256 * c:256 * c + 256], t[:, o:o + LC],
                                        WT4[:, 0:2, :].rearrange("p w m -> p (w m)"), start=True, stop=True)
                elif name == "qb":
                    b = a[0]
                    pe.wait_ge(*at("qs_dve", n, 2 * b + 2))
                    for c in range(CH):
                        ins = pe.transpose(dst[:, LC * c:LC * c + LC], QT[:, b % 2, c, :], ident[0:LC, 0:LC])
                elif name == "kt":
                    b = a[0]
                    pe.wait_ge(*at("exp_act", n, b + 1))
                    for c in range(CH):
                        o = BL * b + LC * c
                        ins = pe.transpose(dst[0:LC, 128 * c:128 * c + 128], keys[:, o:o + LC], ident[:, :])
                elif name == "sq":
                    b = a[0]
                    pe.wait_ge(*at("exp_act", n, NB + b + 1))
                    ins = pe.matmul(dst[:, 0:BL], head_mask[:, :], Q[:, BL * b:BL * b + BL], start=True, stop=True)
                elif name == "ctx":
                    for free in drained(n, ("kt", NB - 1), ("kt", NB - 2), by=(name,) + a):
                        pe.wait_ge(*free)
                    for c in range(NCH):
                        ins = pe.matmul(dst[:, 0:128], VT[0:LC, c, :], KT[0:LC, c, :],
                                        start=(c == 0), stop=(c == NCH - 1))
                elif name == "m":
                    for free in drained(n, ("ctx",), by=(name,) + a):
                        pe.wait_ge(*free)
                    ins = pe.matmul(dst[:, 0:128], ctx_m[:, :], WT4[:, 3, :], start=True, stop=True)
                elif name == "out":
                    b = a[0]
                    for free in drained(n, ("m",), by=(name,) + a):
                        pe.wait_ge(*free)
                    pe.wait_ge(*at("qmul_pool", n, b + 1))
                    ins = pe.matmul(dst[:, 0:BL], mix[:, :], Q[:, BL * b:BL * b + BL], start=True, stop=True)
                elif name == "xf":
                    b, g = a
                    pe.wait_ge(*at("hl_pool", n, b + 1))
                    for j in range(*JG[g]):
                        o = 128 * (j - JG[g][0])
                        ins = pe.transpose(dst[:, o:o + 128], xhl[:, b % 2, j, :, :].rearrange("p a c -> p (a c)"),
                                           ident[:, :])
                elif name == "lg":
                    b = a[0]
                    for free in drained(n, ("xf", b, 0), ("xf", b, 1), by=(name,) + a):
                        pe.wait_ge(*free)
                    for j in range(JB):
                        t = xT[:, JB * b + j, :]
                        pe.matmul(dst[:, E * j:E * j + E], t, Wghi[:, :], start=True, stop=False)
                        ins = pe.matmul(dst[:, E * j:E * j + E], t, Wglo[:, :], start=False, stop=True)
                elif name == "wt":
                    b, g = a
                    pe.wait_ge(*at("gate_dve", n, 20 * b + 20))
                    for j in range(*JG[g]):
                        o = 128 * (j - JG[g][0])
                        ins = pe.transpose(dst[0:32, o:o + 128], w32[:, b % 2, j, :], ident[:, :])
                ins.then_inc(full, 1)

            def hidden(n, s):
                b, q = divmod(s, NQ)
                pe.wait_ge(*at("h_ready", n, s - 1))
                if s % NQ == 0:
                    for free in drained(n, ("xf", b, 0), ("xf", b, 1)):
                        pe.wait_ge(*free)
                for part, w in enumerate((W1hi, W1lo)):
                    for i in range(2):
                        ins = pe.matmul(psum[:, 2 * (s % 2) + i, 0:BL], w[:, 128 * q:128 * q + 128],
                                        xT[:, JB * b:JB * b + JB, 64 * i:64 * i + 64],
                                        start=(part == 0), stop=(part == 1))
                ins.then_inc(S["h_full"], 1)

            def wb(n, b, e):
                k = FFN_FILLS.index(("wb", b, e))
                pe.wait_ge(*at("ffn_free", n, k))
                if e == 0:
                    for free in drained(n, ("wt", b, 0), ("wt", b, 1)):
                        pe.wait_ge(*free)
                pe.matmul(psum[:, FB, 0:BL], sel[:, e, :], wT[:, JB * b:JB * b + JB, :], start=True, stop=True) \
                    .then_inc(S["ffn_full"], 1)

            def ffn(n, name, *a):
                if name == "ffn":
                    b, q = a
                    s = b * NQ + q
                    if s == 0:
                        hidden(n, 0)
                        wb(n, 0, 0)
                    if s + 1 < NB * NQ:
                        hidden(n, s + 1)
                    if q % 2 == 0 and (b, q // 2) != (NB - 1, E - 1):
                        x = b * E + q // 2 + 1
                        wb(n, x // E, x % E)
                    pe.wait_ge(*at("h_ready", n, s + 1))
                    if q % 2 == 0:
                        pe.wait_ge(*at("y_free", n, b * E + q // 2))
                    for i in range(2):
                        ins = pe.matmul(psum[64 * i:64 * i + 64, YB, 0:BL], W2s[:, q, :], h_sb[:, s % HB, i, :],
                                        start=(q % 2 == 0), stop=(q % 2 == 1))
                    ins.then_inc(S["h_used"], 1)
                elif name == "fin":
                    b = a[0]
                    k = FFN_FILLS.index((name,) + a)
                    pe.wait_ge(*at("ffn_free", n, k))
                    pe.wait_ge(*at("acc_added", n, (E - 1) * (b + 1)))
                    sums = acc[:, b % 2, :, :].rearrange("p j t -> p (j t)")
                    for j in range(0, JB, 2):
                        m = min(128, BL - 64 * j)
                        ins = pe.transpose(psum[0:m, FB, 64 * j:64 * j + 128], sums[:, 64 * j:64 * j + m],
                                           ident[:, :])
                    ins.then_inc(S["ffn_full"], 1)

            turns(pe, pre, ffn)

        @block.vector
        def _(dve):
            count = 0

            def const(ins, hold=True):
                nonlocal count
                count += 1
                ins.then_inc(S["consts_dve"], 1)
                if hold:
                    dve.wait_ge(S["consts_dve"], count)

            const(dve.memset(raw_kt[:, :, :], 0.0))
            const(dve.memset(conv_y[:, :], 0.0))
            const(dve.memset(mhalf[:, :], -0.5))
            const(dve.memset(euler[:, :], 2.718281828459045))
            const(dve.memset(w32[:, :, :, :], 0.0))
            for e in range(E):
                const(dve.memset(rev[:, e:e + 1], float(E - e)))
            const(dve.memset(wT[:, :, :].bitcast(F32), 0.0))
            dve.wait_ge(S["consts_pool"], POOL_CONSTS)
            const(dve.tensor_copy(sel[:, :, :], sel_raw))
            dve.wait_ge(S["weights_loaded"], 16 * WEIGHT_LOADS)
            for hi, lo, raw in ((W1hi, W1lo, w1_raw), (Wghi, Wglo, wg_raw)):
                const(dve.tensor_copy(hi[:, :], raw))
                const(dve.tensor_tensor(lo[:, :], raw, hi[:, :].bitcast(F32), ALU.subtract))
            const(dve.tensor_scalar(conv_abs, conv_raw, -1.0, None, ALU.mult))
            const(dve.tensor_tensor(conv_abs, conv_abs, conv_raw, ALU.max))
            const(dve.tensor_scalar(conv_abs, conv_abs, CONV_EPS, None, ALU.add))
            const(dve.reciprocal(conv_abs, conv_abs))
            const(dve.tensor_scalar(conv_raw, conv_raw, 1.0 + CONV_EPS, None, ALU.mult))
            const(dve.tensor_tensor(conv_w[:, :, :], conv_raw, conv_abs, ALU.mult))
            dve.wait_ge(S["weights_t"], 1)
            const(dve.tensor_copy(WT4[:, :, :], psum[:, 0, :].rearrange("p (w m) -> p w m", w=4)))
            assert count == DVE_CONSTS

            def ln(n, name, layer, b):
                k = layer * NB + b
                r = k % 2
                src = x_tok[:, JB * b:JB * b + JB, :]
                xc = ln_x[:, r, :, :]
                st = ln_s[:, r, :, :]

                def done(ins):
                    ins.then_inc(S["ln_dve"], 1)

                if name == "ln_a":
                    if layer == 0:
                        for free in drained(n, ("yt", b, 0), ("yt", b, 1)):
                            dve.wait_ge(*free)
                    else:
                        for free in drained(n, ("out", b)):
                            dve.wait_ge(*free)
                    done(dve.tensor_reduce(st[:, 0, :], src, AX.X, ALU.add))
                    dve.wait_ge(*at("ln_dve", n, 6 * k + 1))
                    done(dve.tensor_scalar(st[:, 1, :], st[:, 0, :], -1.0 / C, None, ALU.mult))
                    dve.wait_ge(*at("ln_dve", n, 6 * k + 2))
                    if k >= 2 and k - 2 < NB:
                        dve.wait_ge(*filled(n, "qv", k - 2, 1))
                    elif k >= 2:
                        dve.wait_ge(*at("hl_pool", n, k - 2 - NB + 1))
                    else:
                        dve.wait_ge(*at("hl_pool", n - 1, NB - 1 + k))
                    done(dve.tensor_tensor(xc, src, st[:, 1, :].unsqueeze(2).to_broadcast([128, JB, C]), ALU.add))
                elif name == "ln_b":
                    dve.wait_ge(*at("ln_pool", n, 2 * k + 1))
                    done(dve.tensor_reduce(st[:, 2, :], ln_sq[:, :, :], AX.X, ALU.add))
                    dve.wait_ge(*at("ln_dve", n, 6 * k + 4))
                    done(dve.tensor_scalar(st[:, 3, :], st[:, 2, :], 1.0 / C, EPS, ALU.mult, ALU.add))
                else:
                    dve.wait_ge(*at("ln_pool", n, 2 * k + 2))
                    done(dve.tensor_tensor(xc, xc, st[:, 4, :].unsqueeze(2).to_broadcast([128, JB, C]), ALU.mult))

            def gate(n, name, b):
                steps = 0 if name == "gate_a" else 12

                def done(ins):
                    nonlocal steps
                    steps += 1
                    ins.then_inc(S["gate_dve"], 1)
                    dve.wait_ge(*at("gate_dve", n, 20 * b + steps))

                def each(k):
                    return gs7[:, k, :].unsqueeze(2).to_broadcast([128, JB, E])

                rv = rev[:, :].unsqueeze(1).to_broadcast([128, JB, E])
                logits, t, one, two, rest = (lg[:, k, :, :] for k in range(5))
                if name == "gate_a":
                    for free in drained(n, ("lg", b)):
                        dve.wait_ge(*free)
                    done(dve.tensor_reduce(gs7[:, 0, :], logits, AX.X, ALU.max))
                    done(dve.tensor_tensor(t, logits, each(0), ALU.is_equal))
                    done(dve.tensor_tensor(t, t, rv, ALU.mult))
                    done(dve.tensor_reduce(gs7[:, 1, :], t, AX.X, ALU.max))
                    done(dve.tensor_tensor(one, t, each(1), ALU.is_equal))
                    done(dve.scalar_tensor_tensor(rest, one, NEG, logits, ALU.mult, ALU.add))
                    done(dve.tensor_reduce(gs7[:, 2, :], rest, AX.X, ALU.max))
                    done(dve.tensor_tensor(t, rest, each(2), ALU.is_equal))
                    done(dve.tensor_tensor(t, t, rv, ALU.mult))
                    done(dve.tensor_reduce(gs7[:, 3, :], t, AX.X, ALU.max))
                    done(dve.tensor_tensor(two, t, each(3), ALU.is_equal))
                    done(dve.tensor_tensor(gs7[:, 4, :], gs7[:, 2, :], gs7[:, 0, :], ALU.subtract))
                else:
                    dve.wait_ge(*at("gate_pool", n, b + 1))
                    done(dve.tensor_scalar(gs7[:, 6, :], gs7[:, 5, :], 1.0, None, ALU.add))
                    done(dve.reciprocal(gs7[:, 7, :], gs7[:, 6, :]))
                    done(dve.tensor_tensor(gs7[:, 8, :], gs7[:, 5, :], gs7[:, 7, :], ALU.mult))
                    done(dve.tensor_tensor(one, one, each(7), ALU.mult))
                    done(dve.tensor_tensor(two, two, each(8), ALU.mult))
                    done(dve.tensor_tensor(t, one, two, ALU.add))
                    if b >= 2:
                        dve.wait_ge(*filled(n, "wt", b - 2, 1))
                    else:
                        dve.wait_ge(*filled(n - 1, "wt", 6 - b, 1))
                    hi = w32[:, b % 2, :, 0:E]
                    done(dve.tensor_copy(hi.bitcast(F32R), t))
                    done(dve.tensor_tensor(w32[:, b % 2, :, E:2 * E].bitcast(F32R), t, hi, ALU.subtract))

            def pre(n, name, *a):
                if name in ("ln_a", "ln_b", "ln_c"):
                    ln(n, name, *a)
                    return
                if name in ("gate_a", "gate_b"):
                    gate(n, name, *a)
                    return
                fill = (name,) + a
                if name == "stats":
                    for free in drained(n, ("tx", 1, 6), ("tx", 1, 5)):
                        dve.wait_ge(*free)
                    for i in range(2):
                        for r in range(NB):
                            ins = dve.bn_stats(bns[:, i, r, :], xpad[:, i, ROWS * r:ROWS * r + ROWS, 1:1 + HW])
                        ins.then_inc(S["gn_dve"], 1)
                    dve.wait_ge(*at("gn_dve", n, 2))
                    dve.memset(xpad[:, :, :, 0:1], 0.0)
                    for i in range(2):
                        dve.bn_aggr(gn[:, 2 * i:2 * i + 2], bns[:, i, :, :].rearrange("p a b -> p (a b)")) \
                            .then_inc(S["gn_dve"], 1)
                elif name == "gs":
                    dve.wait_ge(*filled(n, name))
                    src = bank_of(name)
                    dve.tensor_copy(gn[:, 4:12], src[:, 0:8]).then_inc(pre_free(fill), 1)
                    for free in drained(n, (name,)):
                        dve.wait_ge(*free)
                    means = gn[:, 4:8].rearrange("p (i s) -> p i s", s=2)
                    diffs = gn[:, 8:12].rearrange("p (i s) -> p i s", s=2)
                    v = gn[:, 12:14]
                    dve.tensor_tensor(v, diffs[:, :, 0], diffs[:, :, 0], ALU.mult).then_inc(S["gn_dve"], 1)
                    dve.wait_ge(*at("gn_dve", n, 5))
                    dve.scalar_tensor_tensor(v, v, EPS, means[:, :, 1], ALU.add, ALU.add).then_inc(S["gn_dve"], 1)
                    dve.wait_ge(*at("gn_pool", n, 1))
                    dve.scalar_tensor_tensor(gn[:, 16:18], means[:, :, 0], -1.0, gn[:, 14:16],
                                             ALU.mult, ALU.mult).then_inc(S["gn_dve"], 1)
                elif name == "norm":
                    dve.wait_ge(*at("gn_dve", n, 7))
                    for r in range(0, HW, 14):
                        for i in range(2):
                            part = xpad[:, i, r:r + 14, 1:1 + HW]
                            ins = dve.tensor_scalar(part, part, gn[:, 14 + i:15 + i], gn[:, 16 + i:17 + i],
                                                    ALU.mult, ALU.add)
                            if r == 0:
                                ins.then_inc(S["gn_dve"], 1)
                    dve.memset(xpad[:, :, :, PADW - 1:PADW], 0.0)
                    dve.memset(xpad[:, :, HW:PADH, 1:1 + HW], 0.0)
                    dve.wait_ge(*at("gn_dve", n, 9))
                    dve.memset(xpad[0:64, :, 0:1, 1:1 + HW], 0.0).then_inc(S["gn_dve"], 1)
                elif name == "yt":
                    b, g = a
                    j0, j1 = JG[g]
                    dve.wait_ge(*filled(n, name, b, g))
                    src = bank_of(name, b, g)
                    if (b, g) == (0, 0):
                        dve.wait_ge(*at("x_loaded", n, 16))
                    for i in range(2):
                        h = slice(64 * i, 64 * i + 64)
                        t = x_tok[h, JB * b + j0:JB * b + j1, :]
                        part = src[0:64, 0:128 * (j1 - j0)].rearrange("p (j m) -> p j m", m=128)[:, :, h]
                        ins = dve.tensor_tensor(t, part, t, ALU.add)
                    ins.then_inc(pre_free(fill), 1)
                elif name == "k":
                    b = a[0]
                    dve.wait_ge(*filled(n, name, b))
                    src = bank_of(name, b)
                    dve.tensor_scalar(keys[:, BL * b:BL * b + BL], src[:, 0:BL], bkr[:, 0:1], None,
                                      ALU.add, ALU.max, accum_out=kst[:, 0, b:b + 1]).then_inc(pre_free(fill), 1)
                elif name == "qv":
                    b, g = a
                    dve.wait_ge(*filled(n, name, b, g))
                    src = bank_of(name, b, g)
                    part = src[0:LC, :].rearrange("p (c w m) -> p c w m", c=2, w=2)
                    bias = bqv[:, :].rearrange("p (w m) -> p w m", w=2)
                    c0 = CH * b + 2 * g
                    if g == 0:
                        if b >= 2:
                            dve.wait_ge(*filled(n, "qb", b - 2))
                        else:
                            dve.wait_ge(*filled(n - 1, "qb", 6 - b))
                    dve.tensor_tensor(QT[:, b % 2, 2 * g:2 * g + 2, :], part[:, :, 0, :],
                                      bias[:, 0, :].unsqueeze(1).to_broadcast([LC, 2, 128]), ALU.add)
                    dve.tensor_tensor(VT[0:LC, c0:c0 + 2, :], part[:, :, 1, :],
                                      bias[:, 1, :].unsqueeze(1).to_broadcast([LC, 2, 128]), ALU.add) \
                        .then_inc(pre_free(fill), 1)
                elif name == "qs":
                    b = a[0]
                    for free in drained(n, ("qv", b, 0), ("qv", b, 1)):
                        dve.wait_ge(*free)
                    q = QT[:, b % 2, :, :].rearrange("p c (g k) -> p (c g) k", k=GROUPS)
                    dve.tensor_reduce(q_max[:, b % 2, :], q, AX.X, ALU.max).then_inc(S["qs_dve"], 1)
                    dve.wait_ge(*at("qs_dve", n, 2 * b + 1))
                    dve.tensor_tensor(q, q, q_max[:, b % 2, :].unsqueeze(2).to_broadcast([LC, CH * 16, GROUPS]),
                                      ALU.subtract).then_inc(S["qs_dve"], 1)
                elif name == "hl":
                    b = a[0]
                    k = NB + b
                    dve.wait_ge(*at("ln_dve", n, 6 * k + 6))
                    if b >= 2:
                        dve.wait_ge(*filled(n, "xf", b - 2, 1))
                    else:
                        dve.wait_ge(*filled(n - 1, "xf", 6, 1))
                    dve.tensor_copy(xhl[:, b % 2, :, 0, :].bitcast(F32R), ln_x[:, k % 2, :, :]) \
                        .then_inc(S["hi_dve"], 1)
                elif name == "res":
                    b = a[0]
                    dve.wait_ge(*at("ffn_free", n - 1, FFN_FILLS.index(("fin", b)) + 1))
                    for free in drained(n, ("out", b)):
                        dve.wait_ge(*free)
                    js = slice(JB * b, JB * b + JB)
                    dve.tensor_copy(res[:, js, :], x_tok[:, js, :]).then_inc(S["res_copied"], 1)
                elif name == "kmax":
                    for free in drained(n, ("k", NB - 1), ("k", NB - 2)):
                        dve.wait_ge(*free)
                    dve.tensor_reduce(kred[:, 0:1], kst[:, 0, :], AX.X, ALU.max, negate=True) \
                        .then_inc(S["kmax_dve"], 1)
                elif name == "kt":
                    b = a[0]
                    dve.wait_ge(*filled(n, name, b))
                    src = bank_of(name, b)
                    dve.tensor_copy(KT[0:LC, CH * b:CH * b + CH, :], src[0:LC, :].rearrange(
                        "p (c m) -> p c m", c=CH)).then_inc(pre_free(fill), 1)
                elif name == "sq":
                    b = a[0]
                    dve.wait_ge(*filled(n, name, b))
                    src = bank_of(name, b)
                    dve.wait_ge(*at("qmul_pool", n, b - 1))
                    dve.reciprocal(q_rec[:, b % 2, :], src[:, 0:BL]).then_inc(pre_free(fill), 1)
                elif name == "ksum":
                    dve.wait_ge(*at("exp_act", n, NB))
                    dve.tensor_reduce(kred[:, 1:2], kst[:, 1, :], AX.X, ALU.add).then_inc(S["kmax_dve"], 1)
                    dve.wait_ge(*at("kmax_dve", n, 2))
                    dve.reciprocal(kred[:, 2:3], kred[:, 1:2]).then_inc(S["kmax_dve"], 1)
                elif name == "ctx":
                    dve.wait_ge(*filled(n, name))
                    src = bank_of(name)
                    dve.tensor_tensor(ctx_m[:, :], src[:, 0:128], head_mask[:, :], ALU.mult).then_inc(pre_free(fill), 1)
                elif name == "m":
                    dve.wait_ge(*filled(n, name))
                    src = bank_of(name)
                    dve.wait_ge(*at("kmax_dve", n, 3))
                    dve.tensor_scalar(mix[:, :], src[:, 0:128], kred[:, 2:3], None, ALU.mult).then_inc(pre_free(fill), 1)
                elif name == "out":
                    b = a[0]
                    dve.wait_ge(*filled(n, name, b))
                    src = bank_of(name, b)
                    t = x_tok[:, JB * b:JB * b + JB, :].rearrange("p j c -> p (j c)")
                    dve.scalar_tensor_tensor(t, src[:, 0:BL], bkr[:, 1:2], t, ALU.add, ALU.add) \
                        .then_inc(pre_free(fill), 1)
                elif name == "lg":
                    b = a[0]
                    dve.wait_ge(*filled(n, name, b))
                    src = bank_of(name, b)
                    dve.tensor_tensor(lg[:, 0, :, :], src[:, 0:JB * E].rearrange("p (j e) -> p j e", e=E),
                                      bg_sb[:, :].unsqueeze(1).to_broadcast([128, JB, E]), ALU.add) \
                        .then_inc(pre_free(fill), 1)
                elif name == "wt":
                    b, g = a
                    j0, j1 = JG[g]
                    dve.wait_ge(*filled(n, name, b, g))
                    src = bank_of(name, b, g)
                    if b < NB - 1:
                        dve.wait_ge(*at("ffn_full", n - 1, FFN_FILLS.index(("wb", b, E - 1)) + 1))
                    else:
                        dve.wait_ge(*at("ffn_full", n, 0))
                    for i in range(2):
                        h = slice(64 * i, 64 * i + 64)
                        part = src[0:32, 0:128 * (j1 - j0)].rearrange("p (j m) -> p j m", m=128)[:, :, h]
                        ins = dve.tensor_copy(wT[64 * i:64 * i + 32, JB * b + j0:JB * b + j1, :], part)
                    ins.then_inc(pre_free(fill), 1)

            def ffn(n, name, *a):
                if name == "y":
                    b, e = a
                    dve.wait_ge(*at("h_used", n, NQ * b + 2 * e + 2))
                    dve.wait_ge(*at("ffn_free", n, FFN_FILLS.index(("wb", b, e)) + 1))
                    if e == 0:
                        if b >= 2:
                            dve.wait_ge(*at("ffn_full", n, FFN_FILLS.index(("fin", b - 2)) + 1))
                        else:
                            dve.wait_ge(*at("ffn_full", n, 0))
                        dst = acc[:, b % 2, :, :].rearrange("p j c -> p (j c)")
                    else:
                        prev = (E - 1) * b + e - 2 if e >= 3 else (E - 1) * b
                        dve.wait_ge(*at("acc_added", n, prev))
                        dst = y_tmp[:, e % 2, :]
                    dve.scalar_tensor_tensor(dst, psum[:, YB, 0:BL], b2T[:, e:e + 1], wb_sb[:, e % 2, :],
                                             ALU.add, ALU.mult).then_inc(S["y_free"], 1)
                elif name == "fin":
                    b = a[0]
                    k = FFN_FILLS.index((name,) + a)
                    dve.wait_ge(*at("ffn_full", n, k + 1))
                    dve.wait_ge(*at("res_copied", n, b + 1))
                    dve.wait_ge(*at(f"out_stored{b % 2}", n, 16 * (b // 2)))
                    for i in range(2):
                        h = slice(64 * i, 64 * i + 64)
                        for odd in range(2):
                            part = psum[64 * odd:64 * odd + 64, FB, :].rearrange("p (j m) -> p j m", m=128)
                            ins = dve.tensor_tensor(out_sb[h, b % 2, odd:JB:2, :],
                                                    part[:, 0:(JB + 1 - odd) // 2, h],
                                                    res[h, JB * b + odd:JB * b + JB:2, :], ALU.add)
                    ins.then_inc(S["ffn_free"], 1)

            turns(dve, pre, ffn)


WEIGHT_LOADS = 2 * 12 + 4
POOL_CONSTS = 5 + 2 + 8 + 4
DVE_CONSTS = 6 + E + 1 + 4 + 6 + 1

_INS = ['x', 'L0_conv_kernel', 'L1_attn_Wk', 'L1_attn_bk', 'L1_attn_Wq', 'L1_attn_bq', 'L1_attn_Wv', 'L1_attn_bv',
        'L1_attn_Wr', 'L1_attn_br', 'L1_ffn_Wg', 'L1_ffn_bg', 'L1_ffn_W1', 'L1_ffn_b1', 'L1_ffn_W2', 'L1_ffn_b2']


def kernel(**inputs):
    import numpy as np
    import concourse.bacc as bacc
    from concourse import mybir as mb
    from concourse.bass_utils import run_bass_kernel_spmd

    nc = bacc.Bacc("TRN2", target_bir_lowering=False, num_devices=1)
    arrays, args = {}, []
    for name in _INS:
        a = np.ascontiguousarray(inputs[name])
        arrays[f"in_{name}"] = a
        args.append(nc.dram_tensor(f"in_{name}", a.shape, mb.dt.from_np(a.dtype), kind="ExternalInput").ap())
    args.append(nc.dram_tensor("out_0", (IMAGES, HW, HW, C), mb.dt.float32, kind="ExternalOutput").ap())
    build_program(nc, *args)
    r = run_bass_kernel_spmd(nc, [arrays], core_ids=[0])
    return r.results[0]["out_0"]
```

```python
from contextlib import ExitStack

import concourse.bass as bass
from concourse import mybir

F32 = mybir.dt.float32
F32R = mybir.dt.float32r
ALU = mybir.AluOpType
ACT = mybir.ActivationFunctionType
AX = mybir.AxisListType

IMAGES, HW, C = 32, 56, 64
PAIRS = IMAGES // 2
TOKENS = HW * HW
J = TOKENS // 64
NB = 7
JB = J // NB
BL = JB * 64
ROWS = HW // NB
TQ, TR = 112, 28
LC = 112
CH = BL // LC
NCH = NB * CH
PADW, PADH = HW + 2, HW + 1
E, HID = 8, 256
NQ = E * HID // 128
HB = 4
EPS = 1e-5
CONV_EPS = 0.001
GROUPS = 64 // 8
NEG = -3.0e38
JG = ((0, 4), (4, 7))


def plan():
    steps = []

    def at(slot, name, *args, behind=0):
        steps.append((round(slot, 3), len(steps), name, args, behind))

    for s in range(NB * NQ):
        b, q = divmod(s, NQ)
        at(s, "ffn", b, q, behind=1)
        if q % 2 == 1:
            at(s, "y", b, q // 2, behind=1)
        if q == 0 and b >= 1:
            at(s + 4.4, "fin", b - 1, behind=1)
    last = NB * NQ
    at(last, "start")
    at(last + .1, "start_wb")
    at(last + .3, "fin", NB - 1, behind=1)

    def second(b, s, behind=0):
        at(s, "ln_a", 1, b, behind=behind)
        at(s + 0.6, "ln_sq", 1, b, behind=behind)
        at(s + 1, "ln_b", 1, b, behind=behind)
        at(s + 2.5, "ln_c", 1, b, behind=behind)
        at(s + 2.5, "hl", b, behind=behind)
        at(s + 5, "xf", b, 0, behind=behind)
        at(s + 5.5, "xf", b, 1, behind=behind)
        at(s + 7.4, "lg", b, behind=behind)
        at(s + 7.8, "gate_a", b, behind=behind)
        at(s + 9.1, "gate_b", b, behind=behind)
        at(s + 10.5, "gate_c", b, behind=behind)
        at(s + 11.1, "gate_d", b, behind=behind)
        at(s + 14, "wt", b, 0, behind=behind)
        at(s + 16.5, "wt", b, 1, behind=behind)

    for k in range(14):
        s = 6 + 0.6 * k
        at(s, "tx", k // 7, k % 7)
        if k in (3, 6):
            at(s, "raw_free", 0, k // 6)
    for k in range(8):
        at(12 + 4.5 * (k // 4) + 0.7 * (k % 4), "stats", k // 4, k % 4)
    at(20, "gs")
    at(20, "gs_end")
    for r in range(4):
        at(20 + 0.8 * r, "norm", r)
    for b in range(NB):
        at(22.5 + 2 * b, "cv", b)
    for b in range(NB):
        s = 38 + 3 * b
        at(s, "yt", b, 0)
        at(s, "yt", b, 1)
        at(s + 1, "ln_a", 0, b)
        at(s + 1.1, "ln_sq", 0, b)
        at(s + 1.5, "ln_b", 0, b)
        at(s + 2.8, "ln_c", 0, b)
        k, qv0, qv1, qs = (4.1, 4.6, 5.2, 6.3) if b < NB - 1 else (4.1, 4.8, 4.85, 4.9)
        at(s + k, "k", b)
        at(s + qv0, "qv", b, 0)
        at(s + qv1, "qv", b, 1)
        at(s + qs, "qs", b)
    at(60.11, "kmax")
    at(60.12, "exp")
    for b in range(NB):
        at(61.5 + 0.02 * b, "kt", b)
        at(62.5 + 1.4 * b, "qn", b)
    at(62.5, "ksum")
    at(65.9, "ctx")
    at(67, "m")
    for b in range(NB):
        at(70.5 + 2.75 * b, "qb", b)
        at(74 + 2.75 * b, "out", b)
    for b, s in enumerate((75, 81, 87, 93, 19, 23, 27)):
        second(b, s, behind=int(b >= FIRST_BEHIND))
    for b, s in enumerate((91, 97, 97, 98, 98, 102, 113)):
        at(s, "res", b)
    steps.sort(key=lambda x: (x[0], x[1]))
    return [(name, args, behind) for _, _, name, args, behind in steps]


FIRST_BEHIND = 4
SCHEDULE = plan()
PRE_KINDS = ("tx", "gs", "cv", "yt", "k", "qv", "qb", "kt", "ctx", "m", "out", "xf", "lg", "wt", "fin")
FILLS = [(s[0],) + s[1] for s in SCHEDULE if s[0] in PRE_KINDS]
BEHIND = {(s[0],) + s[1]: s[2] for s in SCHEDULE if s[0] in PRE_KINDS}
FILLS_FIRST = [f for f in FILLS if not BEHIND[f]]
FILLS_LAST = [f for f in FILLS if BEHIND[f]]
assert len(FILLS) % 2 == 0 and len(FILLS_FIRST) % 2 == 0


def build_program(nc, x, conv, Wk, bk, Wq, bq, Wv, bv, Wr, br, Wg, bg, W1, b1, W2, b2, out):
    ctx = ExitStack()
    with ctx:
        def sb(name, shape, dt=F32):
            return ctx.enter_context(nc.sbuf_tensor(name, shape, dt))

        def sem(name):
            return ctx.enter_context(nc.semaphore(name))

        x_tok = sb("x_tok", [128, J, C])
        raw_kt = sb("raw_kt", [128, TR, 128])
        pad_qv = sb("pad_qv", [128, 2 * NCH * 128])
        xpad = pad_qv[:, 0:2 * PADH * PADW].rearrange("p (i r w) -> p i r w", i=2, r=PADH)
        QT = pad_qv[:, 0:NCH * 128].rearrange("p (h k) -> p h k", k=128)
        VT = pad_qv[:, NCH * 128:].rearrange("p (h k) -> p h k", k=128)
        conv_y = sb("conv_y", [128, TOKENS])
        keys = sb("keys", [128, TOKENS])
        ln_x = sb("ln_x", [128, 2, JB, C])
        ln_sq = sb("ln_sq", [128, JB, C])
        ln_s = sb("ln_s", [128, 2, 5, JB])
        Q = sb("Q", [128, 2, BL])
        q_max = sb("q_max", [LC, CH * 16])
        q_sum = sb("q_sum", [LC, 2, CH * 16])
        xhl = sb("xhl", [128, 2, JB, 2, C])
        xT = sb("xT", [128, J, 128], F32R)
        wT = sb("wT", [128, J, 64], F32R)
        res = sb("res", [128, J, C])
        h_sb = sb("h_sb", [128, HB, 2, BL])
        wb_sb = sb("wb_sb", [128, 2, BL])
        y_tmp = sb("y_tmp", [128, 2, BL])
        acc = sb("acc", [128, 2, JB, 64])
        out_sb = sb("out_sb", [128, 2, JB, C])
        W1hi = sb("W1hi", [128, E * HID], F32R)
        W1lo = sb("W1lo", [128, E * HID], F32R)
        W2s = sb("W2s", [128, NQ, C])
        Wg2 = sb("Wg2", [128, 2, E], F32R)
        conv_w = sb("conv_w", [128, 6, C])
        WT4 = sb("WT4", [128, 4, 128])
        sel = sb("sel", [128, E, 128], F32R)
        ident = sb("ident", [128, 128])
        head_mask = sb("head_mask", [128, 128])
        pair_mean = sb("pair_mean", [128, 128])
        pair_diff = sb("pair_diff", [128, 128])
        ctx_m = sb("ctx_m", [128, 128])
        mix = ctx_m
        bqv = sb("bqv", [LC, 256])
        bkr = sb("bkr", [128, 2])
        b1T = sb("b1T", [128, NQ])
        b2T = sb("b2T", [128, E])
        bg_sb = sb("bg_sb", [128, E])
        rev = sb("rev", [128, E])
        bns = sb("bns", [128, 2, NB, 6])
        gn = sb("gn", [128, 20])
        mhalf = sb("mhalf", [128, JB])
        euler = sb("euler", [128, JB])
        kst = sb("kst", [128, NB])
        kred = sb("kred", [128, 3])
        lg = sb("lg", [128, 5, JB, E])
        gs7 = sb("gs7", [128, 9, JB])
        w32 = sb("w32", [128, 2, JB, 32])
        w1_raw = keys[:, 0:E * HID]
        sel_raw = conv_y[:, 0:E * 128].rearrange("p (e m) -> p e m", e=E)
        w_raw = conv_y[:, E * 128:E * 128 + 512].rearrange("p (w m) -> p w m", w=4)
        conv_raw = conv_y[:, 1536:1536 + 384].rearrange("p (w m) -> p w m", w=6)
        conv_abs = conv_y[:, 1920:1920 + 384].rearrange("p (w m) -> p w m", w=6)
        wg_raw = conv_y[:, 2304:2304 + E]
        KT = raw_kt

        psum = ctx.enter_context(nc.psum_tensor("psum", [128, 8, 512], F32))
        PRE0, YBS, FB = 4, (3, 6), 7

        def sems(names):
            return {name: sem(name) for name in names.split()}

        S = sems("weights_loaded consts_pool consts_dve weights_t x_loaded0 x_loaded1 raw_loaded00 raw_loaded01 raw_loaded10 raw_loaded11 "
                 "pre_full0 pre_full1 pre_free0 pre_free1 wb_full wb_free "
                 "h_full h_ready h_used y_free acc_added out_stored0 out_stored1 res_copied "
                 "gn_dve gn_pool ln_dve ln_pool ln_act hi_dve hl_pool qs_dve kmax_dve exp_act qmul_pool "
                 "gate_dve lg_dve gate_pool")

        PER = dict(x_loaded0=16, x_loaded1=16, raw_loaded00=32, raw_loaded01=32, raw_loaded10=32, raw_loaded11=32,
                   wb_full=NB * E, wb_free=NB * E,
                   h_full=2 * NB * NQ, h_ready=2 * NB * NQ, h_used=NB * NQ, y_free=NB * E,
                   acc_added=NB * (E - 1), out_stored0=16 * 4, out_stored1=16 * 3, res_copied=NB,
                   gn_dve=12, gn_pool=1, ln_dve=2 * NB * 5, ln_pool=2 * NB, ln_act=2 * NB, hi_dve=NB, hl_pool=NB,
                   qs_dve=4 * NB, kmax_dve=2, exp_act=2, qmul_pool=NB,
                   gate_dve=20 * NB, lg_dve=NB, gate_pool=NB)

        def at(name, n, c):
            value = n * PER[name] + max(c, 0)
            return S[name], max(value, 0) if isinstance(value, int) else value

        def place(n, fill):
            turn = n + BEHIND[fill]
            before = len(FILLS_FIRST) // 2 + (turn - 1) * (len(FILLS) // 2)
            fills = FILLS
            if isinstance(turn, int) and turn <= 0:
                before, fills = 0, FILLS_FIRST
            elif isinstance(turn, int) and turn == PAIRS:
                fills = FILLS_LAST
            k = fills.index(fill)
            return k % 2, before + k // 2

        def bank_of(n, *fill):
            return psum[:, PRE0 + place(n, fill)[0], :]

        def filled(n, *fill):
            if isinstance(n, int) and n < 0:
                return S["pre_full0"], 0
            bank, before = place(n, fill)
            return S[f"pre_full{bank}"], before + 1

        def empty(n, *fill):
            bank, before = place(n, fill)
            return S[f"pre_free{bank}"], before

        def emptied(n, *fill):
            if isinstance(n, int) and n < 0:
                return S["pre_free0"], 0
            bank, before = place(n, fill)
            return S[f"pre_free{bank}"], before + 1

        def drained(n, *fills, by=None):
            last = {}
            for fill in sorted(fills, key=FILLS.index):
                bank, before = place(n, fill)
                last[bank] = before + 1
            return [(S[f"pre_free{bank}"], value) for bank, value in last.items()
                    if by is None or place(n, by)[0] != bank]

        def latest(kind, n, steps):
            last = {}
            for offset, fill in sorted(steps, key=lambda s: (s[0] + BEHIND[s[1]], FILLS.index(s[1]))):
                if not (isinstance(n, int) and n + offset < 0):
                    bank, before = place(n + offset, fill)
                    last[bank] = before + 1
            return [(S[f"{kind}{bank}"], value) for bank, value in last.items()]

        def all_filled(n, *steps):
            return latest("pre_full", n, steps)

        def all_drained(n, *steps):
            return latest("pre_free", n, steps)

        def pre_free(n, fill):
            return S[f"pre_free{place(n, fill)[0]}"]

        xp = x.rearrange("(n i) h w c -> n i (h w c)", i=2)
        op = out.rearrange("(n i) h w c -> n i (h w c)", i=2)

        def turns(eng, pre, ffn):
            def turn(n, front, back):
                for name, args, behind in SCHEDULE:
                    if (behind and back) or (not behind and front):
                        step = ffn if name in ("ffn", "y", "start", "start_wb") else pre
                        if step is not None:
                            step(n - behind, name, *args)

            turn(0, True, False)
            turn(1, True, True)
            with eng.Fori(2, PAIRS) as n:
                turn(n, True, True)
            turn(PAIRS, False, True)

        block = ctx.enter_context(nc.Block())

        @block.sync
        def _(sp):
            def row(n):
                return n if isinstance(n, int) else bass.ds(n, 1)

            def pre(n, name, *a):
                if name == "tx" and a == (0, 0):
                    if isinstance(n, int) and n == 0:
                        sp.wait_ge(S["consts_dve"], 1)
                    sp.wait_ge(*filled(n - 1, "ctx"))
                    load_raw_at(n, 0, 0)
                    load_raw_at(n, 0, 1)
                if name == "gs":
                    sp.wait_ge(*at("res_copied", n - 1, NB))
                    load_tok_at(n, 0, 0, JB * FIRST_BEHIND)
                if name == "cv" and a == (NB - 1,):
                    sp.wait_ge(*at("ln_dve", n, 0))
                    load_tok_at(n, 1, JB * FIRST_BEHIND, J)
                if name == "raw_free":
                    sp.wait_ge(*filled(n, "tx", 0, 3 if a[1] == 0 else 6))
                    load_raw_at(n, 1, a[1])
                if name == "fin":
                    b = a[0]
                    sp.wait_ge(*emptied(n, "fin", b))
                    dst = op[row(n)]
                    if not isinstance(n, int):
                        dst = dst.rearrange("o i m -> (o i) m")
                    dst = dst.rearrange("i (p j c) -> (i p) j c", p=64, c=C)
                    sp.dma_start(dst[:, JB * b:JB * b + JB, :], out_sb[:, b % 2, :, :]).then_inc(S[f"out_stored{b % 2}"], 16)

            def load_raw_at(n, i, part):
                src = xp[row(n), i]
                if not isinstance(n, int):
                    src = src.rearrange("o m -> (o m)")
                r = slice(16 * part, min(16 * part + 16, TR))
                body = src.rearrange("(q r c) -> q r c", q=TQ, r=TR)
                loaded = S[f"raw_loaded{i}{part}"]
                sp.dma_start(raw_kt[0:TQ, r, 64:128], body[:, r]).then_inc(loaded, 16)
                sp.dma_start(raw_kt[2:TQ, r, 0:64], body[0:TQ - 2, r]).then_inc(loaded, 16)

            def load_tok_at(n, part, j0, j1):
                src = xp[row(n)]
                if not isinstance(n, int):
                    src = src.rearrange("o i m -> (o i) m")
                src = src.rearrange("i (p j c) -> (i p) j c", p=64, c=C)
                sp.dma_start(x_tok[:, j0:j1, :], src[:, j0:j1, :]) \
                    .then_inc(S[f"x_loaded{part}"], 16)

            turns(sp, pre, None)
            sp.wait_ge(*at("out_stored0", PAIRS, 0))
            sp.wait_ge(*at("out_stored1", PAIRS, 0))

        @block.gpsimd
        def _(pool):
            count = 0

            def const(ins):
                nonlocal count
                count += 1
                ins.then_inc(S["consts_pool"], 1)
                pool.wait_ge(S["consts_pool"], count)

            const(pool.memset(ident[:, :], 0.0))
            const(pool.affine_select(out=ident[:, :], in_=ident[:, :], compare_op=ALU.not_equal, fill=1.0,
                                     base=0, pattern=[[-1, 128]], channel_multiplier=1))
            const(pool.memset(head_mask[:, :], 1.0))
            hm = head_mask[:, :].rearrange("p (g k) -> p g k", k=GROUPS)
            const(pool.affine_select(out=hm, in_=hm, compare_op=ALU.is_ge, fill=0.0, base=0,
                                     pattern=[[-GROUPS, 16], [0, GROUPS]], channel_multiplier=1))
            const(pool.affine_select(out=hm, in_=hm, compare_op=ALU.is_ge, fill=0.0, base=GROUPS - 1,
                                     pattern=[[GROUPS, 16], [0, GROUPS]], channel_multiplier=-1))
            const(pool.memset(pair_mean[:, :], 0.0))
            const(pool.memset(pair_diff[:, :], 0.0))
            for m, signs in ((pair_mean, (0.5, 0.5)), (pair_diff, (0.5, -0.5))):
                for half in range(2):
                    for u in range(2):
                        v = m[64:128, 64 * half:64 * half + 64].rearrange("p (g u) -> p g u", u=2)
                        const(pool.affine_select(out=v, in_=v, compare_op=ALU.not_equal, fill=signs[u], base=-u,
                                                 pattern=[[-2, 32], [0, 2]], channel_multiplier=1))
            pool.wait_ge(S["consts_dve"], 2)
            for i in range(2):
                for part in range(2):
                    v = sel_raw[64 * i:64 * i + 64, :, 64 * i:64 * i + 64]
                    const(pool.affine_select(out=v, in_=v, compare_op=ALU.not_equal, fill=1.0, base=-E * part,
                                             pattern=[[-1, E], [0, 64]], channel_multiplier=1))
            assert count == POOL_CONSTS

            def ln_at(layer, b):
                return layer * NB + b

            def pre(n, name, *a):
                if name == "gs_end":
                    pool.wait_ge(*at("gn_dve", n, 6))
                    pool.tensor_tensor(gn[:, 14:16], gn[:, 12:14], mhalf[:, 0:2], ALU.pow).then_inc(S["gn_pool"], 1)
                elif name == "ln_b":
                    k = ln_at(*a)
                    pool.wait_ge(*at("ln_dve", n, 5 * k + 4))
                    pool.tensor_tensor(ln_s[:, k % 2, 4, :], ln_s[:, k % 2, 3, :], mhalf[:, :], ALU.pow) \
                        .then_inc(S["ln_pool"], 1)
                elif name == "hl":
                    b = a[0]
                    k = ln_at(1, b)
                    pool.wait_ge(*at("hi_dve", n, b + 1))
                    pool.tensor_tensor(xhl[:, b % 2, :, 1, :].bitcast(F32R), ln_x[:, k % 2, :, :],
                                       xhl[:, b % 2, :, 0, :], ALU.subtract).then_inc(S["hl_pool"], 1)
                elif name == "qn":
                    b = a[0]
                    pool.wait_ge(*at("qs_dve", n, 2 * NB + 2 * b + 2))
                    q = QT[0:LC, CH * b:CH * b + CH, :].rearrange("p c (g k) -> p (c g) k", k=GROUPS)
                    pool.tensor_tensor(q, q, q_sum[:, b % 2, :].unsqueeze(2).to_broadcast(
                        [LC, CH * 16, GROUPS]), ALU.mult).then_inc(S["qmul_pool"], 1)
                elif name == "gate_b":
                    b = a[0]
                    pool.wait_ge(*at("gate_dve", n, 20 * b + 12))
                    pool.tensor_tensor(gs7[:, 5, :], euler[:, :], gs7[:, 4, :], ALU.pow).then_inc(S["gate_pool"], 1)

            def ffn(n, name, *a):
                if name == "y" and a[1] >= 1:
                    b, e = a
                    pool.wait_ge(*at("y_free", n, b * E + e + 1))
                    pool.wait_ge(*at("acc_added", n, b * (E - 1) + e - 1))
                    s = acc[:, b % 2, :, :].rearrange("p j c -> p (j c)")
                    pool.tensor_tensor(s, s, y_tmp[:, e % 2, :], ALU.add).then_inc(S["acc_added"], 1)

            turns(pool, pre, ffn)

        @block.scalar
        def _(act):
            loads = 0

            def load(dst, src):
                nonlocal loads
                act.dma_start(dst, src, allow_slow_non_contiguous=True).then_inc(S["weights_loaded"], 16)
                loads += 1

            act.wait_ge(S["consts_dve"], 2)
            for i in range(2):
                h = slice(64 * i, 64 * i + 64)
                for w, mat in enumerate((Wq, Wv, Wk, Wr)):
                    load(w_raw[h, w, h], mat)
                load(w1_raw[h, :].rearrange("d (e h) -> d e h", e=E), W1.rearrange("e d h -> d e h"))
                load(wg_raw[h, :], Wg)
                load(bkr[h, 0:1], bk.rearrange("(c o) -> c o", o=1))
                load(bkr[h, 1:2], br.rearrange("(c o) -> c o", o=1))
                load(b2T[h, :], b2.rearrange("e c -> c e"))
                load(bqv[:, h], bq.unsqueeze(0).to_broadcast([LC, 64]))
                load(bqv[:, 128 + 64 * i:192 + 64 * i], bv.unsqueeze(0).to_broadcast([LC, 64]))
                load(conv_raw[h, 0:3, :], conv[i].rearrange("x ci co -> ci x co"))
            load(conv_raw[64:128, 3:6, :], conv[2].rearrange("x ci co -> ci x co"))
            load(W2s[:, :, :], W2.rearrange("e (k p) c -> p (e k) c", p=128))
            load(b1T[:, :], b1.rearrange("e (k p) -> p (e k)", p=128))
            load(bg_sb[:, :], bg.unsqueeze(0).to_broadcast([128, E]))
            assert loads == WEIGHT_LOADS

            def pre(n, name, *a):
                fill = (name,) + a
                if name == "ln_sq":
                    k = a[0] * NB + a[1]
                    act.wait_ge(*at("ln_dve", n, 5 * k + 2))
                    act.activation(ln_sq[:, :, :], ln_x[:, k % 2, :, :], ACT.Square).then_inc(S["ln_act"], 1)
                elif name == "tx":
                    i, g = a
                    src = bank_of(n, name, *a)
                    used = [(-1, ("qb", NB - 1)), (-1, ("ctx",))] if a == (0, 0) else []
                    for full in all_filled(n, (0, fill), *used):
                        act.wait_ge(*full)
                    dst = xpad[:, i, 0:HW, 1:1 + HW].rearrange("p r (h q) -> p r h q", h=2)[:, :, :, 4 * g:4 * g + 4]
                    act.copy(dst, src[:, 0:448].rearrange("p (k r h) -> p r h k", k=4, h=2)) \
                        .then_inc(pre_free(n, (name,) + a), 1)
                elif name == "cv":
                    b = a[0]
                    src = bank_of(n, name, b)
                    used = [(-1, ("yt", NB - 1, 1))] if b == 0 else []
                    for full in all_filled(n, (0, fill), *used):
                        act.wait_ge(*full)
                    act.activation(conv_y[:, BL * b:BL * b + BL], src[:, 0:BL], ACT.Relu) \
                        .then_inc(pre_free(n, (name,) + a), 1)
                elif name == "qb":
                    b = a[0]
                    for full in all_filled(n, (0, fill), *([(0, ("out", b - 2))] if b >= 2 else [])):
                        act.wait_ge(*full)
                    src = bank_of(n, name, b)
                    act.copy(Q[:, b % 2, :], src[:, 0:BL]).then_inc(pre_free(n, (name,) + a), 1)
                elif name == "exp":
                    act.wait_ge(*at("kmax_dve", n, 1))
                    act.activation(keys[:, :], keys[:, :], ACT.Exp, bias=kred[:, 0:1], accum_out=kred[:, 1:2]) \
                        .then_inc(S["exp_act"], 1)
                    act.wait_ge(*at("qs_dve", n, 2 * NB))
                    qt = QT[0:LC, :, :].rearrange("p h k -> p (h k)")
                    act.activation(qt, qt, ACT.Exp).then_inc(S["exp_act"], 1)
                elif name == "xf":
                    b, g = a
                    j0, j1 = JG[g]
                    act.wait_ge(*filled(n, name, b, g))
                    src = bank_of(n, name, b, g)
                    act.wait_ge(*at("h_full", n - 1, 2 * NQ * (b + 1)))
                    act.copy(xT[:, JB * b + j0:JB * b + j1, :], src[:, 0:128 * (j1 - j0)].rearrange(
                        "p (j t) -> p j t", t=128)).then_inc(pre_free(n, (name,) + a), 1)

            def wb(n, b, e):
                act.wait_ge(*at("wb_full", n, b * E + e + 1))
                act.wait_ge(*at("y_free", n, b * E + e - 1))
                act.copy(wb_sb[:, e % 2, :], psum[:, FB, 0:BL]).then_inc(S["wb_free"], 1)

            def gelu(n, s):
                if isinstance(n, int) and n == 0 and s == 0:
                    act.wait_ge(S["weights_loaded"], 16 * WEIGHT_LOADS)
                act.wait_ge(*at("h_used", n, s + 1 - HB))
                for i in range(2):
                    k = 2 * s + i
                    act.wait_ge(*at("h_full", n, k + 1))
                    act.activation(h_sb[:, s % HB, i, :], psum[:, k % 3, 0:BL], ACT.Gelu,
                                   bias=b1T[:, s % NQ:s % NQ + 1]).then_inc(S["h_ready"], 1)

            def ffn(n, name, *a):
                if name == "start":
                    gelu(n, 0)
                elif name == "start_wb":
                    wb(n, 0, 0)
                if name == "ffn":
                    b, q = a
                    s = b * NQ + q
                    if s + 1 < NB * NQ:
                        gelu(n, s + 1)
                    if q % 2 == 0 and (b, q // 2) != (NB - 1, E - 1):
                        x = b * E + q // 2 + 1
                        wb(n, x // E, x % E)

            turns(act, pre, ffn)

        @block.tensor
        def _(pe):
            pe.wait_ge(S["consts_pool"], POOL_CONSTS)

            def prepare_weights():
                pe.wait_ge(S["weights_loaded"], 16 * WEIGHT_LOADS)
                for w in range(4):
                    ins = pe.transpose(psum[:, 0, 128 * w:128 * w + 128], w_raw[:, w, :], ident[:, :])
                ins.then_inc(S["weights_t"], 1)
                pe.wait_ge(S["consts_dve"], DVE_CONSTS)

            def pre(n, name, *a):
                if name not in PRE_KINDS:
                    return
                if name == "gs" and isinstance(n, int) and n == 0:
                    prepare_weights()
                dst, full = bank_of(n, name, *a), S[f"pre_full{place(n, (name,) + a)[0]}"]
                pe.wait_ge(*empty(n, name, *a))
                if name == "tx":
                    i, g = a
                    if g in (0, 4):
                        pe.wait_ge(*at(f"raw_loaded{i}{g // 4}", n, 32))
                    for r in range(4):
                        ins = pe.transpose(dst[:, TQ * r:TQ * r + TQ], raw_kt[0:TQ, 4 * g + r, :],
                                           ident[0:TQ, 0:TQ])
                elif name == "gs":
                    pe.wait_ge(*at("gn_dve", n, 4))
                    pe.matmul(dst[:, 0:4], pair_mean[:, :], gn[:, 0:4], start=True, stop=True)
                    ins = pe.matmul(dst[:, 4:8], pair_diff[:, :], gn[:, 0:4], start=True, stop=True)
                elif name == "cv":
                    b = a[0]
                    last_row = min(ROWS * b + ROWS, HW - 1)
                    pe.wait_ge(*at("gn_dve", n, 9 + last_row // 14))
                    for t in range(6):
                        r0, dx = ROWS * b + t // 3, t % 3
                        for i in range(2):
                            ins = pe.matmul(dst[64 * i:64 * i + 64, 0:BL], conv_w[:, t, :],
                                            xpad[:, i, r0:r0 + ROWS, dx:dx + HW], start=(t == 0), stop=(t == 5))
                elif name == "yt":
                    b, g = a
                    for free in drained(n, ("cv", NB - 2), ("cv", NB - 1), by=(name,) + a):
                        pe.wait_ge(*free)
                    cols = conv_y[:, :].rearrange("k (p j) -> k j p", j=J)
                    for j in range(*JG[g]):
                        o = 128 * (j - JG[g][0])
                        if o == 0:
                            ins = pe.matmul(dst[0:64, o:o + 128], cols[:, JB * b + j, :], ident[:, :],
                                            start=True, stop=True)
                        else:
                            ins = pe.transpose(dst[0:64, o:o + 128], cols[:, JB * b + j, :], ident[:, :])
                elif name == "k":
                    b = a[0]
                    pe.wait_ge(*at("ln_dve", n, 5 * b + 5))
                    ins = pe.matmul(dst[:, 0:BL], WT4[:, 2, :], ln_x[:, b % 2, :, :].rearrange("p j c -> p (j c)"),
                                    start=True, stop=True)
                elif name == "qv":
                    b, g = a
                    pe.wait_ge(*at("ln_dve", n, 5 * b + 5))
                    t = ln_x[:, b % 2, :, :].rearrange("p j c -> p (j c)")
                    for c in range(2):
                        o = LC * (2 * g + c)
                        ins = pe.matmul(dst[0:LC, 256 * c:256 * c + 256], t[:, o:o + LC],
                                        WT4[:, 0:2, :].rearrange("p w m -> p (w m)"), start=True, stop=True)
                elif name == "qb":
                    b = a[0]
                    pe.wait_ge(*at("qmul_pool", n, b + 1))
                    for c in range(CH):
                        ins = pe.transpose(dst[:, LC * c:LC * c + LC], QT[0:LC, CH * b + c, :],
                                           ident[0:LC, 0:LC])
                elif name == "kt":
                    b = a[0]
                    pe.wait_ge(*at("exp_act", n, 1))
                    for c in range(CH):
                        o = BL * b + LC * c
                        ins = pe.transpose(dst[0:LC, 128 * c:128 * c + 128], keys[:, o:o + LC], ident[:, :])
                elif name == "ctx":
                    for free in drained(n, ("kt", NB - 2), ("kt", NB - 1), by=(name,) + a):
                        pe.wait_ge(*free)
                    for c in range(NCH):
                        ins = pe.matmul(dst[:, 0:128], VT[0:LC, c, :], KT[0:LC, c, :],
                                        start=(c == 0), stop=(c == NCH - 1))
                elif name == "m":
                    for free in drained(n, ("ctx",), by=(name,) + a):
                        pe.wait_ge(*free)
                    ins = pe.matmul(dst[:, 0:128], ctx_m[:, :], WT4[:, 3, :], start=True, stop=True)
                elif name == "out":
                    b = a[0]
                    for free in drained(n, ("m",), ("qb", b), by=(name,) + a):
                        pe.wait_ge(*free)
                    ins = pe.matmul(dst[:, 0:BL], mix[:, :], Q[:, b % 2, :], start=True, stop=True)
                elif name == "xf":
                    b, g = a
                    pe.wait_ge(*at("hl_pool", n, b + 1))
                    for j in range(*JG[g]):
                        o = 128 * (j - JG[g][0])
                        ins = pe.transpose(dst[:, o:o + 128], xhl[:, b % 2, j, :, :].rearrange("p a c -> p (a c)"),
                                           ident[:, :])
                elif name == "lg":
                    b = a[0]
                    for free in drained(n, ("xf", b, 0), ("xf", b, 1), by=(name,) + a):
                        pe.wait_ge(*free)
                    for j in range(JB):
                        ins = pe.matmul(dst[:, 2 * E * j:2 * E * j + 2 * E], xT[:, JB * b + j, :],
                                        Wg2[:, :, :].rearrange("p a e -> p (a e)"), start=True, stop=True)
                elif name == "wt":
                    b, g = a
                    pe.wait_ge(*at("gate_dve", n, 20 * b + 20))
                    for j in range(*JG[g]):
                        o = 128 * (j - JG[g][0])
                        ins = pe.transpose(dst[0:32, o:o + 128], w32[:, b % 2, j, :], ident[:, :])
                elif name == "fin":
                    b = a[0]
                    pe.wait_ge(*at("acc_added", n, (E - 1) * (b + 1)))
                    sums = acc[:, b % 2, :, :].rearrange("p j t -> p (j t)")
                    for j in range(0, JB, 2):
                        m = min(128, BL - 64 * j)
                        ins = pe.transpose(dst[0:m, 64 * j:64 * j + 128], sums[:, 64 * j:64 * j + m],
                                           ident[:, :])
                ins.then_inc(full, 1)

            def hidden(n, s):
                b, q = divmod(s, NQ)
                if s % NQ == 0:
                    for free in drained(n, ("xf", b, 0), ("xf", b, 1)):
                        pe.wait_ge(*free)
                for i in range(2):
                    k = 2 * s + i
                    pe.wait_ge(*at("h_ready", n, k - 2))
                    for part, w in enumerate((W1hi, W1lo)):
                        ins = pe.matmul(psum[:, k % 3, 0:BL], w[:, 128 * q:128 * q + 128],
                                        xT[:, JB * b:JB * b + JB, 64 * i:64 * i + 64],
                                        start=(part == 0), stop=(part == 1))
                    ins.then_inc(S["h_full"], 1)

            def wb(n, b, e):
                pe.wait_ge(*at("wb_free", n, b * E + e))
                if e == 0:
                    for free in drained(n, ("wt", b, 0), ("wt", b, 1)):
                        pe.wait_ge(*free)
                pe.matmul(psum[:, FB, 0:BL], sel[:, e, :], wT[:, JB * b:JB * b + JB, :], start=True, stop=True) \
                    .then_inc(S["wb_full"], 1)

            def ffn(n, name, *a):
                if name == "start":
                    hidden(n, 0)
                elif name == "start_wb":
                    wb(n, 0, 0)
                if name == "ffn":
                    b, q = a
                    s = b * NQ + q
                    if s + 1 < NB * NQ:
                        hidden(n, s + 1)
                    if q % 2 == 0 and (b, q // 2) != (NB - 1, E - 1):
                        x = b * E + q // 2 + 1
                        wb(n, x // E, x % E)
                    pe.wait_ge(*at("h_ready", n, 2 * s + 2))
                    if q % 2 == 0:
                        pe.wait_ge(*at("y_free", n, b * E + q // 2 - 1))
                    for i in range(2):
                        ins = pe.matmul(psum[64 * i:64 * i + 64, YBS[q // 2 % 2], 0:BL], W2s[:, q, :], h_sb[:, s % HB, i, :],
                                        start=(q % 2 == 0), stop=(q % 2 == 1))
                    ins.then_inc(S["h_used"], 1)

            turns(pe, pre, ffn)

        @block.vector
        def _(dve):
            count = 0

            def const(ins, hold=True):
                nonlocal count
                count += 1
                ins.then_inc(S["consts_dve"], 1)
                if hold:
                    dve.wait_ge(S["consts_dve"], count)

            const(dve.memset(raw_kt[:, :, :], 0.0))
            const(dve.memset(conv_y[:, :], 0.0))
            const(dve.memset(mhalf[:, :], -0.5))
            const(dve.memset(euler[:, :], 2.718281828459045))
            const(dve.memset(w32[:, :, :, :], 0.0))
            for e in range(E):
                const(dve.memset(rev[:, e:e + 1], float(E - e)))
            const(dve.memset(wT[:, :, :].bitcast(F32), 0.0))
            dve.wait_ge(S["consts_pool"], POOL_CONSTS)
            const(dve.tensor_copy(sel[:, :, :], sel_raw))

            def prepare_weights():
                dve.wait_ge(S["weights_loaded"], 16 * WEIGHT_LOADS)
                for hi, lo, raw in ((W1hi[:, :], W1lo[:, :], w1_raw), (Wg2[:, 0, :], Wg2[:, 1, :], wg_raw)):
                    const(dve.tensor_copy(hi, raw))
                    const(dve.tensor_tensor(lo, raw, hi.bitcast(F32), ALU.subtract))
                const(dve.tensor_scalar(conv_abs, conv_raw, -1.0, None, ALU.mult))
                const(dve.tensor_tensor(conv_abs, conv_abs, conv_raw, ALU.max))
                const(dve.tensor_scalar(conv_abs, conv_abs, CONV_EPS, None, ALU.add))
                const(dve.reciprocal(conv_abs, conv_abs))
                const(dve.tensor_scalar(conv_raw, conv_raw, 1.0 + CONV_EPS, None, ALU.mult))
                const(dve.tensor_tensor(conv_w[:, :, :], conv_raw, conv_abs, ALU.mult))
                dve.wait_ge(S["weights_t"], 1)
                const(dve.tensor_copy(WT4[:, :, :], psum[:, 0, :].rearrange("p (w m) -> p w m", w=4)))
                assert count == DVE_CONSTS

            def ln(n, name, layer, b):
                k = layer * NB + b
                r = k % 2
                src = x_tok[:, JB * b:JB * b + JB, :]
                xc = ln_x[:, r, :, :]
                st = ln_s[:, r, :, :]

                def done(ins):
                    ins.then_inc(S["ln_dve"], 1)

                if name == "ln_a":
                    if layer == 0:
                        for free in drained(n, ("yt", b, 0), ("yt", b, 1)):
                            dve.wait_ge(*free)
                    else:
                        for free in drained(n, ("out", b)):
                            dve.wait_ge(*free)
                    done(dve.tensor_reduce(st[:, 0, :], src, AX.X, ALU.add))
                    dve.wait_ge(*at("ln_dve", n, 5 * k + 1))
                    if k >= 2 and k - 2 < NB:
                        dve.wait_ge(*filled(n, "qv", k - 2, 1))
                    elif k >= 2:
                        dve.wait_ge(*at("hl_pool", n, k - 2 - NB + 1))
                    else:
                        dve.wait_ge(*at("hl_pool", n - 1, NB - 1 + k))
                    done(dve.scalar_tensor_tensor(xc, st[:, 0, :].unsqueeze(2).to_broadcast([128, JB, C]), -1.0 / C, src,
                                                  ALU.mult, ALU.add))
                elif name == "ln_b":
                    dve.wait_ge(*at("ln_act", n, k + 1))
                    done(dve.tensor_reduce(st[:, 2, :], ln_sq[:, :, :], AX.X, ALU.add))
                    dve.wait_ge(*at("ln_dve", n, 5 * k + 3))
                    done(dve.tensor_scalar(st[:, 3, :], st[:, 2, :], 1.0 / C, EPS, ALU.mult, ALU.add))
                else:
                    dve.wait_ge(*at("ln_pool", n, k + 1))
                    done(dve.tensor_tensor(xc, xc, st[:, 4, :].unsqueeze(2).to_broadcast([128, JB, C]), ALU.mult))

            def gate(n, name, b):
                steps = {"gate_a": 0, "gate_b": 5, "gate_c": 12, "gate_d": 18}[name]

                def done(ins):
                    nonlocal steps
                    steps += 1
                    ins.then_inc(S["gate_dve"], 1)
                    dve.wait_ge(*at("gate_dve", n, 20 * b + steps))

                def each(k):
                    return gs7[:, k, :].unsqueeze(2).to_broadcast([128, JB, E])

                rv = rev[:, :].unsqueeze(1).to_broadcast([128, JB, E])
                logits, t, one, two, rest = (lg[:, k, :, :] for k in range(5))
                if name == "gate_a":
                    for free in drained(n, ("lg", b)):
                        dve.wait_ge(*free)
                    done(dve.tensor_reduce(gs7[:, 0, :], logits, AX.X, ALU.max))
                    done(dve.tensor_tensor(t, logits, each(0), ALU.is_equal))
                    done(dve.tensor_tensor(t, t, rv, ALU.mult))
                    done(dve.tensor_reduce(gs7[:, 1, :], t, AX.X, ALU.max))
                    done(dve.tensor_tensor(one, t, each(1), ALU.is_equal))
                elif name == "gate_b":
                    done(dve.scalar_tensor_tensor(rest, one, NEG, logits, ALU.mult, ALU.add))
                    done(dve.tensor_reduce(gs7[:, 2, :], rest, AX.X, ALU.max))
                    done(dve.tensor_tensor(t, rest, each(2), ALU.is_equal))
                    done(dve.tensor_tensor(t, t, rv, ALU.mult))
                    done(dve.tensor_reduce(gs7[:, 3, :], t, AX.X, ALU.max))
                    done(dve.tensor_tensor(two, t, each(3), ALU.is_equal))
                    done(dve.tensor_tensor(gs7[:, 4, :], gs7[:, 2, :], gs7[:, 0, :], ALU.subtract))
                elif name == "gate_c":
                    dve.wait_ge(*at("gate_pool", n, b + 1))
                    done(dve.tensor_scalar(gs7[:, 6, :], gs7[:, 5, :], 1.0, None, ALU.add))
                    done(dve.reciprocal(gs7[:, 7, :], gs7[:, 6, :]))
                    done(dve.tensor_tensor(gs7[:, 8, :], gs7[:, 5, :], gs7[:, 7, :], ALU.mult))
                    done(dve.tensor_tensor(one, one, each(7), ALU.mult))
                    done(dve.tensor_tensor(two, two, each(8), ALU.mult))
                    done(dve.tensor_tensor(t, one, two, ALU.add))
                else:
                    if b >= 2:
                        dve.wait_ge(*filled(n, "wt", b - 2, 1))
                    else:
                        dve.wait_ge(*filled(n - 1, "wt", 6 - b, 1))
                    hi = w32[:, b % 2, :, 0:E]
                    done(dve.tensor_copy(hi.bitcast(F32R), t))
                    done(dve.tensor_tensor(w32[:, b % 2, :, E:2 * E].bitcast(F32R), t, hi, ALU.subtract))

            def pre(n, name, *a):
                if name == "gs" and isinstance(n, int) and n == 0:
                    prepare_weights()
                if name in ("ln_a", "ln_b", "ln_c"):
                    ln(n, name, *a)
                    return
                if name in ("gate_a", "gate_b", "gate_c", "gate_d"):
                    gate(n, name, *a)
                    return
                fill = (name,) + a
                if name == "stats":
                    i, k = a
                    for free in drained(n, ("tx", i, 5), ("tx", i, 6)):
                        dve.wait_ge(*free)
                    if k < 3:
                        for r in range(3 * k, min(3 * k + 3, NB)):
                            ins = dve.bn_stats(bns[:, i, r, :], xpad[:, i, ROWS * r:ROWS * r + ROWS, 1:1 + HW])
                        if k == 2:
                            ins.then_inc(S["gn_dve"], 1)
                    else:
                        dve.memset(xpad[:, i, :, 0:1], 0.0)
                        dve.memset(xpad[:, i, :, PADW - 1:PADW], 0.0)
                        dve.wait_ge(*at("gn_dve", n, 2 * i + 1))
                        dve.memset(xpad[:, i, HW:PADH, 1:1 + HW], 0.0)
                        dve.bn_aggr(gn[:, 2 * i:2 * i + 2], bns[:, i, :, :].rearrange("p a b -> p (a b)")) \
                            .then_inc(S["gn_dve"], 1)
                elif name == "gs":
                    dve.wait_ge(*filled(n, name, *a))
                    dve.tensor_copy(gn[:, 4:12], bank_of(n, name)[:, 0:8]) \
                        .then_inc(pre_free(n, fill), 1)
                elif name == "gs_end":
                    dve.wait_ge(*emptied(n, "gs"))
                    means = gn[:, 4:8].rearrange("p (i s) -> p i s", s=2)
                    diffs = gn[:, 8:12].rearrange("p (i s) -> p i s", s=2)
                    v = gn[:, 12:14]
                    dve.tensor_tensor(v, diffs[:, :, 0], diffs[:, :, 0], ALU.mult).then_inc(S["gn_dve"], 1)
                    dve.wait_ge(*at("gn_dve", n, 5))
                    dve.scalar_tensor_tensor(v, v, EPS, means[:, :, 1], ALU.add, ALU.add).then_inc(S["gn_dve"], 1)
                elif name == "norm":
                    if a[0] == 0:
                        dve.wait_ge(*at("gn_pool", n, 1))
                        dve.scalar_tensor_tensor(gn[:, 16:18], gn[:, 4:8:2], -1.0, gn[:, 14:16],
                                                 ALU.mult, ALU.mult).then_inc(S["gn_dve"], 1)
                        dve.wait_ge(*at("gn_dve", n, 7))
                    for i in range(2):
                        part = xpad[:, i, 14 * a[0]:14 * a[0] + 14, 1:1 + HW]
                        ins = dve.tensor_scalar(part, part, gn[:, 14 + i:15 + i], gn[:, 16 + i:17 + i],
                                                ALU.mult, ALU.add)
                    ins.then_inc(S["gn_dve"], 1)
                    if a[0] == 0:
                        dve.wait_ge(*at("gn_dve", n, 8))
                        dve.memset(xpad[0:64, :, 0:1, 1:1 + HW], 0.0).then_inc(S["gn_dve"], 1)
                elif name == "yt":
                    b, g = a
                    j0, j1 = JG[g]
                    dve.wait_ge(*filled(n, name, b, g))
                    src = bank_of(n, name, b, g)
                    if g == 0 and b in (0, FIRST_BEHIND):
                        dve.wait_ge(*at(f"x_loaded{int(b > 0)}", n, 16))
                    for i in range(2):
                        h = slice(64 * i, 64 * i + 64)
                        t = x_tok[h, JB * b + j0:JB * b + j1, :]
                        part = src[0:64, 0:128 * (j1 - j0)].rearrange("p (j m) -> p j m", m=128)[:, :, h]
                        ins = dve.tensor_tensor(t, part, t, ALU.add)
                    ins.then_inc(pre_free(n, fill), 1)
                elif name == "k":
                    b = a[0]
                    dve.wait_ge(*filled(n, name, b))
                    src = bank_of(n, name, b)
                    dve.tensor_scalar(keys[:, BL * b:BL * b + BL], src[:, 0:BL], bkr[:, 0:1], None,
                                      ALU.add, ALU.max, accum_out=kst[:, b:b + 1]).then_inc(pre_free(n, fill), 1)
                elif name == "qv":
                    b, g = a
                    dve.wait_ge(*filled(n, name, b, g))
                    src = bank_of(n, name, b, g)
                    part = src[0:LC, :].rearrange("p (c w m) -> p c w m", c=2, w=2)
                    bias = bqv[:, :].rearrange("p (w m) -> p w m", w=2)
                    c0 = CH * b + 2 * g
                    dve.tensor_tensor(QT[0:LC, c0:c0 + 2, :], part[:, :, 0, :],
                                      bias[:, 0, :].unsqueeze(1).to_broadcast([LC, 2, 128]), ALU.add)
                    dve.tensor_tensor(VT[0:LC, c0:c0 + 2, :], part[:, :, 1, :],
                                      bias[:, 1, :].unsqueeze(1).to_broadcast([LC, 2, 128]), ALU.add) \
                        .then_inc(pre_free(n, fill), 1)
                elif name == "qs":
                    b = a[0]
                    for free in drained(n, ("qv", b, 0), ("qv", b, 1)):
                        dve.wait_ge(*free)
                    q = QT[0:LC, CH * b:CH * b + CH, :].rearrange("p c (g k) -> p (c g) k", k=GROUPS)
                    dve.tensor_reduce(q_max[:, :], q, AX.X, ALU.max).then_inc(S["qs_dve"], 1)
                    dve.wait_ge(*at("qs_dve", n, 2 * b + 1))
                    dve.tensor_tensor(q, q, q_max[:, :].unsqueeze(2).to_broadcast([LC, CH * 16, GROUPS]),
                                      ALU.subtract).then_inc(S["qs_dve"], 1)
                elif name == "hl":
                    b = a[0]
                    k = NB + b
                    dve.wait_ge(*at("ln_dve", n, 5 * k + 5))
                    if b >= 2:
                        dve.wait_ge(*filled(n, "xf", b - 2, 1))
                    else:
                        dve.wait_ge(*filled(n - 1, "xf", 6, 1))
                    dve.tensor_copy(xhl[:, b % 2, :, 0, :].bitcast(F32R), ln_x[:, k % 2, :, :]) \
                        .then_inc(S["hi_dve"], 1)
                elif name == "res":
                    b = a[0]
                    for free in all_drained(n, (-1, ("fin", b)), (0, ("out", b))):
                        dve.wait_ge(*free)
                    js = slice(JB * b, JB * b + JB)
                    dve.tensor_copy(res[:, js, :], x_tok[:, js, :]).then_inc(S["res_copied"], 1)
                elif name == "kmax":
                    for free in drained(n, ("k", NB - 2), ("k", NB - 1)):
                        dve.wait_ge(*free)
                    dve.tensor_reduce(kred[:, 0:1], kst[:, :], AX.X, ALU.max, negate=True) \
                        .then_inc(S["kmax_dve"], 1)
                elif name == "kt":
                    b = a[0]
                    dve.wait_ge(*filled(n, name, b))
                    src = bank_of(n, name, b)
                    dve.tensor_copy(KT[0:LC, CH * b:CH * b + CH, :], src[0:LC, :].rearrange(
                        "p (c m) -> p c m", c=CH)).then_inc(pre_free(n, fill), 1)
                elif name == "qn":
                    b = a[0]
                    dve.wait_ge(*at("exp_act", n, 2))
                    dve.wait_ge(*at("qmul_pool", n, b - 1))
                    q = QT[0:LC, CH * b:CH * b + CH, :].rearrange("p c (g k) -> p (c g) k", k=GROUPS)
                    dve.tensor_reduce(q_sum[:, b % 2, :], q, AX.X, ALU.add).then_inc(S["qs_dve"], 1)
                    dve.wait_ge(*at("qs_dve", n, 2 * NB + 2 * b + 1))
                    dve.reciprocal(q_sum[:, b % 2, :], q_sum[:, b % 2, :]).then_inc(S["qs_dve"], 1)
                elif name == "ksum":
                    dve.wait_ge(*at("exp_act", n, 1))
                    dve.reciprocal(kred[:, 2:3], kred[:, 1:2]).then_inc(S["kmax_dve"], 1)
                elif name == "ctx":
                    dve.wait_ge(*filled(n, name))
                    src = bank_of(n, name)
                    dve.tensor_tensor(ctx_m[:, :], src[:, 0:128], head_mask[:, :], ALU.mult).then_inc(pre_free(n, fill), 1)
                elif name == "m":
                    dve.wait_ge(*filled(n, name))
                    src = bank_of(n, name)
                    dve.wait_ge(*at("kmax_dve", n, 2))
                    dve.tensor_scalar(mix[:, :], src[:, 0:128], kred[:, 2:3], None, ALU.mult).then_inc(pre_free(n, fill), 1)
                elif name == "out":
                    b = a[0]
                    dve.wait_ge(*filled(n, name, b))
                    src = bank_of(n, name, b)
                    t = x_tok[:, JB * b:JB * b + JB, :].rearrange("p j c -> p (j c)")
                    dve.scalar_tensor_tensor(t, src[:, 0:BL], bkr[:, 1:2], t, ALU.add, ALU.add) \
                        .then_inc(pre_free(n, fill), 1)
                elif name == "lg":
                    b = a[0]
                    dve.wait_ge(*filled(n, name, b))
                    src = bank_of(n, name, b)
                    both = src[:, 0:2 * JB * E].rearrange("p (j a e) -> p j a e", a=2, e=E)
                    dve.tensor_tensor(lg[:, 4, :, :], both[:, :, 0, :],
                                      bg_sb[:, :].unsqueeze(1).to_broadcast([128, JB, E]), ALU.add) \
                        .then_inc(S["lg_dve"], 1)
                    dve.wait_ge(*at("lg_dve", n, b + 1))
                    dve.tensor_tensor(lg[:, 0, :, :], both[:, :, 1, :], lg[:, 4, :, :], ALU.add) \
                        .then_inc(pre_free(n, fill), 1)
                elif name == "wt":
                    b, g = a
                    j0, j1 = JG[g]
                    dve.wait_ge(*filled(n, name, b, g))
                    src = bank_of(n, name, b, g)
                    dve.wait_ge(*at("wb_full", n - 1, E * (b + 1)))
                    for i in range(2):
                        h = slice(64 * i, 64 * i + 64)
                        part = src[0:32, 0:128 * (j1 - j0)].rearrange("p (j m) -> p j m", m=128)[:, :, h]
                        ins = dve.tensor_copy(wT[64 * i:64 * i + 32, JB * b + j0:JB * b + j1, :], part)
                    ins.then_inc(pre_free(n, fill), 1)
                elif name == "fin":
                    b = a[0]
                    dve.wait_ge(*filled(n, name, b))
                    src = bank_of(n, name, b)
                    dve.wait_ge(*at("res_copied", n, b + 1))
                    dve.wait_ge(*at(f"out_stored{b % 2}", n, 16 * (b // 2)))
                    for i in range(2):
                        h = slice(64 * i, 64 * i + 64)
                        for odd in range(2):
                            part = src[64 * odd:64 * odd + 64, :].rearrange("p (j m) -> p j m", m=128)
                            ins = dve.tensor_tensor(out_sb[h, b % 2, odd:JB:2, :],
                                                    part[:, 0:(JB + 1 - odd) // 2, h],
                                                    res[h, JB * b + odd:JB * b + JB:2, :], ALU.add)
                    ins.then_inc(pre_free(n, fill), 1)

            def ffn(n, name, *a):
                if name == "y":
                    b, e = a
                    dve.wait_ge(*at("h_used", n, NQ * b + 2 * e + 2))
                    dve.wait_ge(*at("wb_free", n, b * E + e + 1))
                    if e == 0:
                        if b >= 2:
                            dve.wait_ge(*filled(n, "fin", b - 2))
                        else:
                            dve.wait_ge(*filled(n - 1, "fin", NB - 1 - b))
                        dst = acc[:, b % 2, :, :].rearrange("p j c -> p (j c)")
                    else:
                        prev = (E - 1) * b + e - 2 if e >= 3 else (E - 1) * b
                        dve.wait_ge(*at("acc_added", n, prev))
                        dst = y_tmp[:, e % 2, :]
                    dve.scalar_tensor_tensor(dst, psum[:, YBS[e % 2], 0:BL], b2T[:, e:e + 1], wb_sb[:, e % 2, :],
                                             ALU.add, ALU.mult).then_inc(S["y_free"], 1)

            turns(dve, pre, ffn)


WEIGHT_LOADS = 2 * 12 + 4
POOL_CONSTS = 5 + 2 + 8 + 4
DVE_CONSTS = 6 + E + 1 + 4 + 6 + 1

_INS = ['x', 'L0_conv_kernel', 'L1_attn_Wk', 'L1_attn_bk', 'L1_attn_Wq', 'L1_attn_bq', 'L1_attn_Wv', 'L1_attn_bv',
        'L1_attn_Wr', 'L1_attn_br', 'L1_ffn_Wg', 'L1_ffn_bg', 'L1_ffn_W1', 'L1_ffn_b1', 'L1_ffn_W2', 'L1_ffn_b2']


def kernel(**inputs):
    import numpy as np
    import concourse.bacc as bacc
    from concourse import mybir as mb
    from concourse.bass_utils import run_bass_kernel_spmd

    nc = bacc.Bacc("TRN2", target_bir_lowering=False, num_devices=1)
    arrays, args = {}, []
    for name in _INS:
        a = np.ascontiguousarray(inputs[name])
        arrays[f"in_{name}"] = a
        args.append(nc.dram_tensor(f"in_{name}", a.shape, mb.dt.from_np(a.dtype), kind="ExternalInput").ap())
    args.append(nc.dram_tensor("out_0", (IMAGES, HW, HW, C), mb.dt.float32, kind="ExternalOutput").ap())
    build_program(nc, *args)
    r = run_bass_kernel_spmd(nc, [arrays], core_ids=[0])
    return r.results[0]["out_0"]
```
